# Optimizing a Trainium2 kernel written in Bass

```python
import numpy as np
import jax
import jax.numpy as jnp

def _softmax(x, axis=-1):
    return jax.nn.softmax(x, axis=axis)

def _gelu(x):
    return jax.nn.gelu(x, approximate=True)

def _silu(x):
    return jax.nn.silu(x)

def _sigmoid(x):
    return jax.nn.sigmoid(x)

def _layernorm(x, axis=-1, eps=1e-05):
    m = jnp.mean(x, axis=axis, keepdims=True)
    v = jnp.var(x, axis=axis, keepdims=True)
    return (x - m) / jnp.sqrt(v + eps)

def _scatter_add(tgt, idx, src, axis=0):
    return tgt.at[idx].add(src)

def _segment_sum(src, seg, n):
    return jax.ops.segment_sum(src, seg, n)
kernel_name = 'mk_adj_preln_d1_adj_r2_5f6166'

def setup_inputs(seed: int=0):
    np.random.seed(seed)
    _w = jnp.asarray

    def _rec_inputs():
        import jax
        import jax.numpy as jnp
        _gk = jax.random.key(seed)
        x = 7.22e-05 + 1 * jax.random.normal(jax.random.fold_in(_gk, 1), (64, 128, 1024), jnp.float32)
        _a = jax.random.bernoulli(jax.random.fold_in(_gk, 2), 0.03125, (128, 128))
        _a = jnp.logical_or(_a, jnp.swapaxes(_a, -1, -2))
        _a = jnp.logical_or(_a, jnp.eye(128, dtype=bool))
        _af = _a.astype(jnp.float32)
        _af = _af * jax.random.uniform(jax.random.fold_in(_gk, 3), (128, 128), jnp.float32, 0.05, 0.27663)
        adj = _af
        return (x, adj)
    x, adj = _rec_inputs()

    def _L0_gnn_setup():
        import jax, jax.numpy as jnp
        import numpy as np
        N, B, T = (1024, 16, 128)
        key = jax.random.key(seed)
        k1, k2, k3, k4 = jax.random.split(key, 4)
        x = jax.random.normal(k1, (B, T, N), dtype=jnp.float32)
        weight = jax.random.normal(k2, (T, T), dtype=jnp.float32) * (1.0 / np.sqrt(T))
        bias = jax.random.normal(k3, (T,), dtype=jnp.float32) * 0.01
        u = jax.random.uniform(k4, (N * N, 2), dtype=jnp.float32, minval=1e-06, maxval=1.0 - 1e-06)
        gumbel = -jnp.log(-jnp.log(u))
        return {'x': x, 'weight': weight, 'bias': bias, 'gumbel': gumbel}
    _L0_gnn_all = _L0_gnn_setup()
    _L0_gnn_in = {k: v for k, v in _L0_gnn_all.items() if k in ('bias', 'gumbel')}
    del _L0_gnn_all
    return {'x': x, 'adj': adj, 'L0_gnn_bias': _L0_gnn_in['bias'], 'L0_gnn_gumbel': _L0_gnn_in['gumbel']}

def reference(x, adj, L0_gnn_bias, L0_gnn_gumbel):
    import jax
    import jax.numpy as jnp

    def _L0_gnn_ref(x, weight, bias, gumbel):
        import jax, jax.numpy as jnp
        import numpy as np
        N, B, T = (1024, 16, 128)
        xp = jnp.transpose(x, (2, 0, 1))
        n = xp.shape[0]
        xs = jax.lax.stop_gradient(xp)
        x_avg = xs.mean(axis=1)
        x_norm = x_avg / jnp.maximum(jnp.linalg.norm(x_avg, axis=-1, keepdims=True), 1e-12)
        sim = (x_norm @ x_norm.T + 1.0) * 0.5
        sim_flat = sim.reshape(-1)
        score0 = sim_flat + gumbel[:, 0]
        score1 = 1.0 - sim_flat + gumbel[:, 1]
        adj = (score0 > score1).astype(xp.dtype).reshape(n, n)
        adj_sym = jnp.clip(adj + adj.T, 0.0, 1.0)
        nmask = jnp.clip(adj_sym + jnp.eye(n, dtype=xp.dtype), 0.0, 1.0)
        common = nmask @ nmask.T
        max_common = common.max()
        valid = adj_sym * (common > 1.0).astype(xp.dtype) > 0
        struct = jnp.where(valid, common / max_common * common, 0.0)
        W = adj * struct
        deg = W.sum(axis=0)
        dinv = jnp.where(deg > 0, deg ** (-0.5), 0.0)
        Wn = dinv[:, None] * W * dinv[None, :]
        xw = jnp.einsum('nbt,to->nbo', xp, weight)
        out = jnp.einsum('sd,sbt->dbt', Wn, xw) + bias
        return jnp.transpose(out, (1, 2, 0))
    h = jnp.maximum(_layernorm(x, axis=-1), 0.0)
    x = x + _L0_gnn_ref(h, adj, L0_gnn_bias, L0_gnn_gumbel)
    return x

_drawn_inputs = setup_inputs


def setup_inputs(seed=0):
    import zlib

    import numpy as np

    out = dict(_drawn_inputs(seed))
    spreads = {}
    factors = {'L0_gnn_bias': 6.683, 'L0_gnn_gumbel': 5.902}
    for name, (base, spread) in spreads.items():
        noise = np.random.default_rng([zlib.crc32(name.encode()), seed]).standard_normal(out[name].shape)
        drawn = base * np.exp(spread * noise) if base else spread * noise
        out[name] = jnp.asarray(drawn.astype(out[name].dtype))
    for name, factor in factors.items():
        out[name] = (out[name] * factor).astype(out[name].dtype)
    return out
```

```python
from contextlib import ExitStack

import concourse.bass as bass
from concourse import mybir

ALU = mybir.AluOpType
ACT = mybir.ActivationFunctionType
AX_X = mybir.AxisListType.X
F32 = mybir.dt.float32
F16 = mybir.dt.float16
BF16 = mybir.dt.bfloat16

P = 128
BODY = 8
RESIDENT = (2, 6)
POOL_SUMS = (0, 3, 5)
REST = tuple(j for j in range(BODY) if j not in RESIDENT)
EPS = 1e-5
NORM_MIN = 1e-12
TINY = 1e-30
COMMON_SCALE = 0.125
Y_SCALE = 256.0


def gnn_kernel(nc, x, adj, bias, gumbel, out):
    B, T, N = x.shape
    C = N // P
    H = 512
    TRIPS = B // BODY
    HALF = BODY // 2
    NR, NO = len(RESIDENT), len(REST)
    NP, NT = len(POOL_SUMS), BODY - len(POOL_SUMS)
    TENSOR_SUMS = tuple(j for j in range(BODY) if j not in POOL_SUMS)
    assert T == P and N == 1024 and B % BODY == 0 and NR % 2 == 0 and NO % 2 == 0

    gumbel_rows = gumbel.rearrange("(c p d) g -> c p (d g)", p=P, d=N)
    bias_col = bias.rearrange("(t o) -> t o", o=1)

    with ExitStack() as ctx:
        def sb(name, shape, dt=F32):
            return ctx.enter_context(nc.sbuf_tensor(name, shape, dt))

        def sem(name):
            return ctx.enter_context(nc.semaphore(name))

        xring = sb("xring", [P, BODY, N])
        hring = sb("hring", [P, 4, N])
        work = sb("work", [P, 8, N])
        a16 = sb("a16", [P, 2, C, N], F16)
        xw_res = sb("xw_res", [P, TRIPS * NR, N])
        ident = sb("ident", [P, P])
        ident16 = sb("ident16", [P, P], BF16)
        ones = sb("ones", [P, P])
        ones16 = sb("ones16", [P, 1], F16)
        zeros = sb("zeros", [P, P])
        w = sb("w", [P, P])
        w_abs = sb("w_abs", [P, P])
        w_inv = sb("w_inv", [P, P])
        w_unit = sb("w_unit", [P, P])
        w_sum = sb("w_sum", [P, 1])
        bias_sb = sb("bias_sb", [P, 1])
        stats = sb("stats", [P, 4, 12])
        moments = sb("moments", [P, BODY, 2])
        var_eps = sb("var_eps", [P, 2])
        neg_mean = sb("neg_mean", [P, 2])
        eps = sb("eps", [P, 2])
        minus_one = sb("minus_one", [P, 2])
        neg_half = sb("neg_half", [P, C])
        rstd = sb("rstd", [P, B])
        nbias = sb("nbias", [P, B])
        norm2 = sb("norm2", [P, C])
        rnorm = sb("rnorm", [P, C])
        degree = sb("degree", [P, C])
        has_deg = sb("has_deg", [P, C])
        dinv_raw = sb("dinv_raw", [P, C])
        dinv = sb("dinv", [P, C])
        u = sb("u", [P, C])
        row_f = sb("row_f", [P, C])
        row_count = sb("row_count", [P, C])
        col2 = sb("col2", [P, 2])
        top = sb("top", [1, 2])
        top_b = sb("top_b", [P, 2])
        small = sb("small", [P, 4])

        adjm = xring[:, 0:4, :].bitcast(BF16).rearrange("p a (b n) -> p (a b) n", b=2)
        nmask = xring[:, 4:8, :].bitcast(BF16).rearrange("p a (b n) -> p (a b) n", b=2)
        S, sq, diag, xn = (hring[:, k, :] for k in range(4))
        gum = a16[:, :, :, :].bitcast(F32).rearrange("p k c n -> p (k c n)").rearrange("p (r n) -> p r n", r=4)
        acc = work[:, 7, :]
        sim_s = [work[:, k, :] for k in (0, 1)]
        score0 = [work[:, k, :] for k in (2, 3)]
        nscore1 = [work[:, k, :] for k in (4, 5)]
        com2 = [work[:, k, :] for k in (0, 1)]
        cmask = [work[:, 2, :].bitcast(BF16)[:, k * N:(k + 1) * N] for k in (0, 1)]
        a32 = [work[:, k, :] for k in (3, 4)]
        zbuf = [work[:, k, :] for k in (0, 1)]
        obuf = [work[:, k, :] for k in (2, 3)]
        yhi = [work[:, k, :].bitcast(F16)[:, 0:N] for k in (4, 5)]
        ylo = [work[:, k, :].bitcast(F16)[:, N:2 * N] for k in (4, 5)]
        row_fb = work[:, 6, :]

        ps = ctx.enter_context(nc.psum_tensor("ps", [P, 8, H], F32))
        pair = [ps[:, 2 * k:2 * k + 2, :].rearrange("p a n -> p (a n)") for k in range(4)]
        ps_avg = pair[0]
        ps_xw1 = [pair[1], pair[2]]
        ps_w = ps[:, 7, :]
        ps_norm = ps[:, 6, 0:C]
        ps_bc = pair[1]
        ps_sim = [pair[2], pair[0]]
        ps_sym = [pair[1], pair[3]]
        ps_com = [pair[2], pair[0]]
        ps_deg = ps[:, 2, 0:C]
        ps_top = ps[:, 3, :]
        ps_rowf = pair[3]
        ps_out = [pair[0], pair[1]]
        ps_xw2 = [pair[2], pair[3]]

        s_consts = sem("consts_loaded")
        s_x1 = [sem(f"x1_loaded{j}") for j in range(BODY)]
        s_gum = [sem(f"gumbel_loaded{k}") for k in range(4)]
        s_xr = [sem(f"xr_loaded{k}") for k in range(NR)]
        s_xo = [sem(f"xo_loaded{k}") for k in range(NO)]
        s_store = [sem(f"stored{k}") for k in range(2)]
        s_ident = sem("ident_built")
        s_wabs = sem("w_abs_ready")
        s_wsum = sem("w_sums_ready")
        s_w = sem("w_unit_ready")
        s_wchain = sem("w_chain")
        s_bn = sem("bn_stats_done")
        s_bnseen = sem("bn_stats_seen")
        s_mom = sem("moments_ready")
        s_pchain = sem("pool_chain")
        s_norm = sem("norms_ready")
        s_h = sem("h_ready")
        s_hpe = sem("h_summed_by_tensor")
        s_hpool = sem("h_summed_by_pool")
        s_xw1 = sem("xw1_ready")
        s_xw1used = sem("xw1_stored")
        s_S = sem("S_ready")
        s_sq = sem("sq_ready")
        s_n2 = sem("norm2_ready")
        s_n2s = sem("norm2_in_sbuf")
        s_rn = sem("rnorm_ready")
        s_diag = sem("diag_ready")
        s_bc = sem("rnorm_row_ready")
        s_xn = sem("xn_ready")
        s_sim = sem("sim_ready")
        s_sims = sem("sim_in_sbuf")
        s_sc0 = sem("score0_ready")
        s_sc1 = sem("score1_ready")
        s_adj = sem("adj_ready")
        s_sym = sem("sym_ready")
        s_mask = sem("nmask_ready")
        s_com = sem("common_ready")
        s_com2 = sem("common2_ready")
        s_cm = sem("cmask_ready")
        s_a32 = sem("a32_ready")
        s_ahi = sem("a_high_ready")
        s_alo = sem("a_low_ready")
        s_deg = sem("degree_ready")
        s_dchain = sem("degree_chain")
        s_pow = sem("dinv_raw_ready")
        s_colmax = sem("column_maxima_ready")
        s_topT = sem("maxima_transposed")
        s_top = sem("top_ready")
        s_topb = sem("top_broadcast")
        s_u = sem("u_ready")
        s_diagf = sem("row_factor_diag_ready")
        s_rowp = sem("row_factor_in_psum")
        s_rowf = sem("row_factor_ready")
        s_h2 = sem("h2_ready")
        s_xw2 = sem("xw2_ready")
        s_z = sem("z_ready")
        s_yhi = sem("y_high_ready")
        s_y = sem("y_ready")
        s_mm = sem("product_ready")
        s_scaled = sem("product_scaled")
        s_out = sem("out_ready")

        block = ctx.enter_context(nc.Block())

        ORDER1 = TRIPS * NR

        @block.sync
        def _(sp):
            for q in s_store:
                sp.sem_inc(q, 16)
            sp.dma_start(w[:], adj).then_inc(s_consts, 16)
            sp.dma_start(bias_sb[:], bias_col).then_inc(s_consts, 16)
            for j in range(BODY):
                sp.dma_start(xring[:, j, :], x[j]).then_inc(s_x1[j], 16)
            with sp.Fori(1, TRIPS) as i:
                for j in range(BODY):
                    sp.wait_ge(s_h, BODY * (i - 1) + j + 1)
                    sp.dma_start(xring[:, j, :], x[BODY * i + j]).then_inc(s_x1[j], 16)
            for c in range(C):
                if c >= 4:
                    sp.wait_ge(s_adj, c - 3)
                sp.dma_start(gum[:, c % 4, :], gumbel_rows[c]).then_inc(s_gum[c % 4], 16)

            sp.wait_ge(s_com, C)
            for k, j in enumerate(RESIDENT):
                sp.dma_start(xring[:, NO + k, :], x[j]).then_inc(s_xr[k], 16)
            sp.wait_ge(s_cm, C)
            for k, j in enumerate(REST):
                sp.dma_start(xring[:, k, :], x[j]).then_inc(s_xo[k], 16)

            def store_and_reload(i, k, js, count, slot0, sems, more):
                sp.wait_ge(s_out, count)
                sp.dma_start(out[BODY * i + js[k]], obuf[k % 2]).then_inc(s_store[k % 2], 16)
                if more:
                    sp.dma_start(xring[:, slot0 + k, :], x[BODY * (i + 1) + js[k]]).then_inc(sems[k], 16)

            with sp.Fori(0, TRIPS - 1) as i:
                for k in range(NR):
                    store_and_reload(i, k, RESIDENT, NR * i + k + 1, NO, s_xr, True)
            for k in range(NR):
                store_and_reload(TRIPS - 1, k, RESIDENT, NR * (TRIPS - 1) + k + 1, NO, s_xr, False)
            with sp.Fori(0, TRIPS - 1) as i:
                for k in range(NO):
                    store_and_reload(i, k, REST, ORDER1 + NO * i + k + 1, 0, s_xo, True)
            for k in range(NO):
                store_and_reload(TRIPS - 1, k, REST, ORDER1 + NO * (TRIPS - 1) + k + 1, 0, s_xo, False)
            for q in s_store:
                sp.wait_ge(q, 16 * (B // 2 + 1))

        @block.gpsimd
        def _(pool):
            nc.gpsimd.memset(neg_half[:], -0.5).then_inc(s_pchain, 1)
            nc.gpsimd.memset(eps[:], EPS).then_inc(s_pchain, 1)
            nc.gpsimd.memset(minus_one[:], -1.0).then_inc(s_pchain, 1)
            nc.gpsimd.memset(acc, 0.0).then_inc(s_pchain, 1)
            nc.gpsimd.memset(ones16[:], 1.0).then_inc(s_pchain, 1)
            nc.gpsimd.memset(ones[:], 1.0).then_inc(s_pchain, 1)
            pool.wait_ge(s_pchain, 6)
            nc.gpsimd.affine_select(out=ident[:], in_=ones[:], compare_op=ALU.is_equal, fill=0.0, base=0,
                                    pattern=[[-1, P]], channel_multiplier=1).then_inc(s_ident, 1)
            pool.wait_ge(s_ident, 1)
            nc.gpsimd.tensor_copy(ident16[:], ident[:]).then_inc(s_ident, 1)

            def norms(i, q):
                done = 6 + 3 * (HALF * i + q)
                pool.wait_ge(s_mom, BODY * i + 2 * q + 2)
                nc.gpsimd.tensor_tensor(var_eps[:], moments[:, 2 * q:2 * q + 2, 1], eps[:],
                                        ALU.add).then_inc(s_pchain, 1)
                nc.gpsimd.tensor_tensor(neg_mean[:], moments[:, 2 * q:2 * q + 2, 0], minus_one[:],
                                        ALU.mult).then_inc(s_pchain, 1)
                pool.wait_ge(s_pchain, done + 2)
                r = rstd[:, bass.ds(BODY * i + 2 * q, 2)]
                nc.gpsimd.tensor_tensor(r, var_eps[:], neg_half[:, 0:2], ALU.pow).then_inc(s_pchain, 1)
                pool.wait_ge(s_pchain, done + 3)
                nc.gpsimd.tensor_tensor(nbias[:, bass.ds(BODY * i + 2 * q, 2)], neg_mean[:], r,
                                        ALU.mult).then_inc(s_norm, 1)
                pool.wait_ge(s_norm, HALF * (i + 1) + q + 1)

            def add(i, j):
                k = POOL_SUMS.index(j)
                pool.wait_ge(s_h, BODY * i + j + 1)
                pool.wait_ge(s_hpool, NP * (i + 1) + k)
                nc.gpsimd.tensor_tensor(acc, acc, hring[:, j % 4, :], ALU.add).then_inc(s_hpool, 1)

            pool.sem_inc(s_hpool, NP)
            pool.sem_inc(s_norm, HALF)
            with pool.Fori(0, TRIPS) as i:
                norms(i, 0)
                norms(i, 1)
                for j in range(BODY):
                    if j in POOL_SUMS:
                        add(i, j)
                    if j % 2 == 1 and j // 2 + 2 < HALF:
                        norms(i, j // 2 + 2)

            pool.wait_ge(s_n2s, 1)
            nc.gpsimd.tensor_tensor(rnorm[:], norm2[:], neg_half[:], ALU.pow).then_inc(s_rn, 1)
            for c in range(C):
                pool.wait_ge(s_sims, c + 1)
                pool.wait_ge(s_gum[c % 4], 16 * (c // 4 + 1))
                if c >= 2:
                    pool.wait_ge(s_adj, c - 1)
                nc.gpsimd.tensor_tensor(score0[c % 2], sim_s[c % 2],
                                        gum[:, c % 4, :].rearrange("p (d g) -> p g d", g=2)[:, 0, :],
                                        ALU.add).then_inc(s_sc0, 1)
            for c in range(C):
                pool.wait_ge(s_cm, c + 1)
                pool.wait_ge(s_com2, c + 1)
                if c >= 2:
                    pool.wait_ge(s_alo, c - 1)
                nc.gpsimd.tensor_tensor(a32[c % 2], com2[c % 2], cmask[c % 2], ALU.mult).then_inc(s_a32, 1)
            pool.wait_ge(s_dchain, 4)
            nc.gpsimd.tensor_tensor(dinv_raw[:], degree[:], neg_half[:], ALU.pow).then_inc(s_pow, 1)

        @block.scalar
        def _(act):
            def relu1(i, j):
                act.wait_ge(s_norm, HALF * (i + 1) + j // 2 + 1)
                last = (j + 4) % BODY
                trip = i + 1 if j >= 4 else i
                if last in POOL_SUMS:
                    act.wait_ge(s_hpool, NP * trip + POOL_SUMS.index(last) + 1)
                else:
                    act.wait_ge(s_hpe, NT * trip + TENSOR_SUMS.index(last) + 1)
                t = BODY * i + j
                nc.scalar.activation(hring[:, j % 4, :], xring[:, j, :], ACT.Relu, bias=nbias[:, bass.ds(t, 1)],
                                     scale=rstd[:, bass.ds(t, 1)]).then_inc(s_h, 1)

            def keep(i, k):
                act.wait_ge(s_xw1, NR * i + k + 1)
                nc.scalar.activation(xw_res[:, bass.ds(NR * i + k, 1), :].rearrange("p a n -> p (a n)"),
                                     ps_xw1[k % 2], ACT.Copy).then_inc(s_xw1used, 1)

            act.sem_inc(s_xw1used, 2)
            with act.Fori(0, TRIPS) as i:
                for j in range(BODY):
                    relu1(i, j)
                    if j - 1 in RESIDENT:
                        keep(i, RESIDENT.index(j - 1))

            act.wait_ge(s_S, 1)
            nc.scalar.activation(sq, S, ACT.Square, scale=1.0 / B).then_inc(s_sq, 1)
            for c in range(C):
                act.wait_ge(s_sim, c + 1)
                if c >= 2:
                    act.wait_ge(s_sc0, c - 1)
                    act.wait_ge(s_sc1, c - 1)
                nc.scalar.activation(sim_s[c % 2], ps_sim[c % 2], ACT.Copy, bias=0.5,
                                     scale=0.5).then_inc(s_sims, 1)
            for c in range(C):
                act.wait_ge(s_sym, c + 1)
                nc.scalar.activation(nmask[:, c, :], ps_sym[c % 2], ACT.Sign,
                                     accum_out=row_count[:, c:c + 1]).then_inc(s_mask, 1)

            def high(c):
                act.wait_ge(s_a32, c + 1)
                nc.scalar.activation(a16[:, 0, c, :], a32[c % 2], ACT.Copy).then_inc(s_ahi, 1)

            for c in range(C):
                act.wait_ge(s_com, c + 1)
                if c >= 2:
                    act.wait_ge(s_a32, c - 1)
                nc.scalar.activation(com2[c % 2], ps_com[c % 2], ACT.Square,
                                     scale=COMMON_SCALE).then_inc(s_com2, 1)
                if c >= 1:
                    high(c - 1)
            high(C - 1)

            def relu2(i, k, n):
                act.wait_ge(s_xo[k], 16 * (i + 1))
                act.wait_ge(s_xw2, n + 1)
                t = BODY * i + REST[k]
                nc.scalar.activation(hring[:, k % 2, :], xring[:, k, :], ACT.Relu, bias=nbias[:, bass.ds(t, 1)],
                                     scale=rstd[:, bass.ds(t, 1)]).then_inc(s_h2, 1)

            def y_high(n, k):
                act.wait_ge(s_z, n + 1)
                act.wait_ge(s_mm, n + 1)
                nc.scalar.activation(yhi[k % 2], zbuf[k % 2], ACT.Copy).then_inc(s_yhi, 1)

            with act.Fori(0, TRIPS) as i:
                for k in range(NR):
                    y_high(NR * i + k, k)
            relu2(0, 0, 0)
            relu2(0, 1, 1)
            with act.Fori(0, TRIPS - 1) as i:
                for k in range(NO):
                    y_high(ORDER1 + NO * i + k, k)
                    if k + 2 < NO:
                        relu2(i, k + 2, NO * i + k + 2)
                    else:
                        relu2(i + 1, k + 2 - NO, NO * i + k + 2)
            for k in range(NO):
                y_high(ORDER1 + NO * (TRIPS - 1) + k, k)
                if k + 2 < NO:
                    relu2(TRIPS - 1, k + 2, NO * (TRIPS - 1) + k + 2)

        @block.tensor
        def _(pe):
            pe.sem_inc(s_hpe, NT)
            pe.sem_inc(s_xw2, 2)
            pe.sem_inc(s_mm, 2)
            pe.wait_ge(s_wabs, 1)
            pe.wait_ge(s_ident, 2)
            nc.tensor.matmul(ps_w[:, 0:P], ones[:], w_abs[:], start=True, stop=True)
            nc.tensor.matmul(ps_w[:, P:P + 1], w_abs[:], ones[:, 0:1], start=True, stop=True,
                             skip_group_check=True).then_inc(s_wsum, 1)
            for m in range(2):
                nc.tensor.matmul(ps_avg[:, m * H:m * H + P], zeros[:], ones[:], start=True, stop=True,
                                 skip_group_check=True)

            def xw(h, dst):
                for c in range(C):
                    mm = nc.tensor.matmul(dst[:, c * P:(c + 1) * P], h[:, c * P:(c + 1) * P], w_unit[:],
                                          start=True, stop=True, skip_group_check=True)
                return mm

            def bcast(dst, src):
                for m in range(2):
                    mm = nc.tensor.matmul(dst[:, m * H:(m + 1) * H], ones[:], src[:, m * H:(m + 1) * H],
                                          start=True, stop=True)
                return mm

            pe.wait_ge(s_w, 1)
            with pe.Fori(0, TRIPS) as i:
                for j in range(BODY):
                    h = hring[:, j % 4, :]
                    if j in RESIDENT:
                        k = RESIDENT.index(j)
                        pe.wait_ge(s_h, BODY * i + j + 1)
                        pe.wait_ge(s_xw1used, NR * i + k + 1)
                        xw(h, ps_xw1[k % 2]).then_inc(s_xw1, 1)
                    if j in TENSOR_SUMS:
                        pe.wait_ge(s_h, BODY * i + j + 1)
                        for m in range(2):
                            mm = nc.tensor.matmul(ps_avg[:, m * H:(m + 1) * H], ident[:], h[:, m * H:(m + 1) * H],
                                                  start=False, stop=True, skip_group_check=True)
                        mm.then_inc(s_hpe, 1)

            pe.wait_ge(s_sq, 1)
            for c in range(C):
                mm = nc.tensor.matmul(ps_norm[:, c:c + 1], sq[:, c * P:(c + 1) * P], ones[:, 0:1],
                                      start=True, stop=True, skip_group_check=True)
            mm.then_inc(s_n2, 1)
            pe.wait_ge(s_diag, 1)
            bcast(ps_bc, diag).then_inc(s_bc, 1)
            pe.wait_ge(s_xn, 1)
            for c in range(C):
                if c >= 2:
                    pe.wait_ge(s_sims, c - 1)
                for m in range(2):
                    mm = nc.tensor.matmul(ps_sim[c % 2][:, m * H:(m + 1) * H], xn[:, c * P:(c + 1) * P],
                                          xn[:, m * H:(m + 1) * H], start=True, stop=True)
                mm.then_inc(s_sim, 1)
            pe.wait_ge(s_adj, C)
            for c in range(C):
                if c >= 2:
                    pe.wait_ge(s_mask, c - 1)
                for m in range(2):
                    nc.tensor.matmul(ps_sym[c % 2][:, m * H:(m + 1) * H], ident16[:], adjm[:, c, m * H:(m + 1) * H],
                                     start=True, stop=False, skip_group_check=True)
                for k in range(C):
                    nc.tensor.matmul(ps_sym[c % 2][:, k * P:(k + 1) * P], adjm[:, k, c * P:(c + 1) * P], ident16[:],
                                     start=False, stop=k != c, skip_group_check=True)
                nc.tensor.matmul(ps_sym[c % 2][:, c * P:(c + 1) * P], ident16[:], ident16[:],
                                 start=False, stop=True, skip_group_check=True).then_inc(s_sym, 1)

            def degrees(c):
                pe.wait_ge(s_alo, c + 1)
                for d in range(C):
                    for part in range(2):
                        mm = nc.tensor.matmul(ps_deg[:, d:d + 1], a16[:, part, c, d * P:(d + 1) * P], ones16[:],
                                              start=(c == d == part == 0), stop=(c == C - 1 and part == 1),
                                              skip_group_check=True)
                return mm

            def spread(col, s_in, n, s_done):
                pe.wait_ge(s_in, n + 1)
                nc.tensor.transpose(ps_top[0:1, 0:P], col, ident[:]).then_inc(s_done, 1)
                pe.wait_ge(s_top, n + 1)
                nc.tensor.matmul(ps_top[:, P:P + 1], ones[0:1, :], top[:, n:n + 1], start=True, stop=True,
                                 skip_group_check=True).then_inc(s_topb, 1)

            pe.wait_ge(s_mask, C)
            for c in range(C):
                if c >= 2:
                    pe.wait_ge(s_com2, c - 1)
                for k in range(C):
                    for m in range(2):
                        mm = nc.tensor.matmul(ps_com[c % 2][:, m * H:(m + 1) * H], nmask[:, k, c * P:(c + 1) * P],
                                              nmask[:, k, m * H:(m + 1) * H], start=(k == 0), stop=(k == C - 1))
                mm.then_inc(s_com, 1)
                if c == 1:
                    spread(col2[:, 0:1], s_colmax, 0, s_topT)
                if c >= 2:
                    degrees(c - 2)
            degrees(C - 2)
            degrees(C - 1).then_inc(s_deg, 1)
            spread(col2[:, 1:2], s_colmax, 1, s_topT)

            def product(n, k):
                pe.wait_ge(s_y, n + 3)
                pe.wait_ge(s_scaled, n + 1)
                for c in range(C):
                    cs = slice(c * P, (c + 1) * P)
                    for y, parts in ((yhi, (0, 1)), (ylo, (0,))):
                        for part in parts:
                            for m in range(2):
                                mm = nc.tensor.matmul(ps_out[k % 2][:, m * H:(m + 1) * H], y[k % 2][:, cs],
                                                      a16[:, part, c, m * H:(m + 1) * H],
                                                      start=(c == 0 and y is yhi and part == 0),
                                                      stop=(c == C - 1 and y is ylo))
                mm.then_inc(s_mm, 1)

            def xw_rest(n, k):
                pe.wait_ge(s_h2, n + 1)
                pe.wait_ge(s_z, ORDER1 + n - 1)
                xw(hring[:, k % 2, :], ps_xw2[k % 2]).then_inc(s_xw2, 1)

            pe.wait_ge(s_diagf, 1)
            bcast(ps_rowf, diag).then_inc(s_rowp, 1)
            with pe.Fori(0, TRIPS - 1) as i:
                for k in range(NR):
                    product(NR * i + k, k)
            for k in range(NR):
                if k == NR - 1:
                    xw_rest(0, 0)
                product(NR * (TRIPS - 1) + k, k)
            with pe.Fori(0, TRIPS - 1) as i:
                for k in range(NO):
                    xw_rest(NO * i + k + 1, k + 1)
                    product(ORDER1 + NO * i + k, k)
            for k in range(NO):
                if k < NO - 1:
                    xw_rest(NO * (TRIPS - 1) + k + 1, k + 1)
                product(ORDER1 + NO * (TRIPS - 1) + k, k)

        @block.vector
        def _(dve):
            dve.sem_inc(s_scaled, 2)
            dve.sem_inc(s_y, 2)
            nc.vector.memset(zeros[:], 0.0).then_inc(s_wchain, 1)
            dve.wait_ge(s_consts, 32)
            nc.vector.scalar_tensor_tensor(out=w_abs[:], in0=w[:], scalar=-1.0, in1=w[:], op0=ALU.mult,
                                           op1=ALU.max).then_inc(s_wabs, 1)
            dve.wait_ge(s_wsum, 1)
            nc.vector.tensor_scalar(w_inv[:], ps_w[:, 0:P], TINY, None, ALU.max).then_inc(s_wchain, 1)
            nc.vector.tensor_scalar(w_sum[:], ps_w[:, P:P + 1], TINY, None, ALU.max).then_inc(s_wchain, 1)
            dve.wait_ge(s_wchain, 3)
            nc.vector.reciprocal(w_unit[:], w_inv[:]).then_inc(s_wchain, 1)
            dve.wait_ge(s_wchain, 4)
            nc.vector.tensor_tensor(w_unit[:], w_unit[:], w[:], ALU.mult).then_inc(s_w, 1)

            with dve.Fori(0, TRIPS) as i:
                for q in range(HALF):
                    for j in (2 * q, 2 * q + 1):
                        dve.wait_ge(s_x1[j], 16 * (i + 1))
                        for m in range(2):
                            nc.vector.bn_stats(stats[:, j % 4, 6 * m:6 * m + 6],
                                               xring[:, j, m * H:(m + 1) * H]).then_inc(s_bn, 1)
                    dve.wait_ge(s_norm, HALF * i + q + 1)
                    dve.wait_ge(s_bn, 4 * (HALF * i + q) + 4)
                    dve.sem_inc(s_bnseen, 1)
                    for j in (2 * q, 2 * q + 1):
                        nc.vector.bn_aggr(moments[:, j, :], stats[:, j % 4, :]).then_inc(s_mom, 1)

            dve.wait_ge(s_hpe, NT * (TRIPS + 1))
            dve.wait_ge(s_hpool, NP * (TRIPS + 1))
            nc.vector.tensor_tensor(S, ps_avg, acc, ALU.add).then_inc(s_S, 1)
            dve.wait_ge(s_n2, 1)
            nc.vector.tensor_scalar(norm2[:], ps_norm, NORM_MIN ** 2, None, ALU.max).then_inc(s_n2s, 1)

            def diagonal(col, factor):
                return nc.vector.scalar_tensor_tensor(
                    out=diag.rearrange("p (c n) -> p c n", c=C), in0=ident[:].unsqueeze(1).broadcast_to([P, C, P]),
                    scalar=factor, in1=col[:].unsqueeze(2).broadcast_to([P, C, P]), op0=ALU.mult, op1=ALU.mult)

            dve.wait_ge(s_rn, 1)
            diagonal(rnorm, 1.0 / B).then_inc(s_diag, 1)
            dve.wait_ge(s_bc, 1)
            dve.wait_ge(s_S, 1)
            nc.vector.tensor_tensor(xn, S, ps_bc, ALU.mult).then_inc(s_xn, 1)
            for c in range(C):
                dve.wait_ge(s_sims, c + 1)
                dve.wait_ge(s_gum[c % 4], 16 * (c // 4 + 1))
                if c >= 2:
                    dve.wait_ge(s_adj, c - 1)
                nc.vector.scalar_tensor_tensor(out=nscore1[c % 2], in0=sim_s[c % 2], scalar=1.0,
                                               in1=gum[:, c % 4, :].rearrange("p (d g) -> p g d", g=2)[:, 1, :],
                                               op0=ALU.subtract, op1=ALU.subtract).then_inc(s_sc1, 1)
                dve.wait_ge(s_sc1, c + 1)
                dve.wait_ge(s_sc0, c + 1)
                nc.vector.scalar_tensor_tensor(out=adjm[:, c, :], in0=nscore1[c % 2], scalar=-1.0, in1=score0[c % 2],
                                               op0=ALU.mult, op1=ALU.is_lt).then_inc(s_adj, 1)

            dve.wait_ge(s_mask, C)
            nc.vector.tensor_reduce(col2[:, 0:1], row_count[:], AX_X, ALU.max).then_inc(s_colmax, 1)

            def top_of(n):
                dve.wait_ge(s_topT, n + 1)
                nc.vector.tensor_reduce(top[:, n:n + 1], ps_top[0:1, 0:P], AX_X, ALU.max).then_inc(s_top, 1)

            def low(c):
                dve.wait_ge(s_ahi, c + 1)
                nc.vector.tensor_tensor(a16[:, 1, c, :], a32[c % 2], a16[:, 0, c, :],
                                        ALU.subtract).then_inc(s_alo, 1)

            for c in range(C):
                dve.wait_ge(s_com2, c + 1)
                if c >= 2:
                    dve.wait_ge(s_a32, c - 1)
                nc.vector.scalar_tensor_tensor(out=cmask[c % 2], in0=com2[c % 2], scalar=COMMON_SCALE ** 2,
                                               in1=adjm[:, c, :], op0=ALU.is_gt, op1=ALU.mult).then_inc(s_cm, 1)
                if c == 1:
                    top_of(0)
                    dve.wait_ge(s_topb, 1)
                    nc.vector.tensor_copy(top_b[:, 0:1], ps_top[:, P:P + 1]).then_inc(s_dchain, 1)
                if c >= 1:
                    low(c - 1)
            low(C - 1)
            dve.wait_ge(s_dchain, 1)
            nc.vector.reciprocal(small[:, 0:1], top_b[:, 0:1]).then_inc(s_dchain, 1)
            dve.wait_ge(s_dchain, 2)
            nc.vector.tensor_scalar(small[:, 1:2], small[:, 0:1], COMMON_SCALE ** -2, None,
                                    ALU.mult).then_inc(s_dchain, 1)
            dve.wait_ge(s_dchain, 3)
            dve.wait_ge(s_deg, 1)
            nc.vector.tensor_scalar(degree[:], ps_deg, small[:, 1:2], TINY, ALU.mult, ALU.max).then_inc(s_dchain, 1)
            nc.vector.tensor_scalar(has_deg[:], ps_deg, 0.0, None, ALU.is_gt).then_inc(s_dchain, 1)
            dve.wait_ge(s_pow, 1)
            dve.wait_ge(s_dchain, 5)
            nc.vector.tensor_tensor(dinv[:], dinv_raw[:], has_deg[:], ALU.mult).then_inc(s_dchain, 1)
            dve.wait_ge(s_dchain, 6)
            nc.vector.tensor_reduce(col2[:, 1:2], dinv[:], AX_X, ALU.max).then_inc(s_colmax, 1)
            top_of(1)
            dve.wait_ge(s_topb, 2)
            nc.vector.tensor_scalar(top_b[:, 1:2], ps_top[:, P:P + 1], TINY, None, ALU.max).then_inc(s_dchain, 1)
            dve.wait_ge(s_dchain, 7)
            nc.vector.reciprocal(small[:, 2:3], top_b[:, 1:2]).then_inc(s_dchain, 1)
            dve.wait_ge(s_dchain, 8)
            nc.vector.tensor_scalar(u[:], dinv[:], small[:, 2:3], Y_SCALE, ALU.mult, ALU.mult).then_inc(s_u, 1)
            nc.vector.tensor_scalar(small[:, 3:4], top_b[:, 1:2], small[:, 1:2], 1.0 / Y_SCALE,
                                    ALU.mult, ALU.mult).then_inc(s_dchain, 1)
            dve.wait_ge(s_dchain, 9)
            nc.vector.tensor_scalar(row_f[:], dinv[:], small[:, 3:4], None, ALU.mult).then_inc(s_dchain, 1)
            dve.wait_ge(s_u, 1)

            u_b = u[:].unsqueeze(2).broadcast_to([P, C, P])

            def z_of(n, k, src):
                dve.wait_ge(s_y, n + 1)
                nc.vector.tensor_tensor(zbuf[k % 2].rearrange("p (c t) -> p c t", c=C),
                                        src.rearrange("p (c t) -> p c t", c=C), u_b, ALU.mult).then_inc(s_z, 1)

            def y_low(n, k):
                dve.wait_ge(s_yhi, n + 1)
                nc.vector.tensor_tensor(ylo[k % 2], zbuf[k % 2], yhi[k % 2], ALU.subtract).then_inc(s_y, 1)

            def y_res(n, k):
                z_of(n, k, xw_res[:, bass.ds(n, 1), :].rearrange("p a n -> p (a n)"))
                y_low(n, k)

            def y_rest(n, k):
                dve.wait_ge(s_xw2, n + 3)
                z_of(ORDER1 + n, k, ps_xw2[k % 2])
                y_low(ORDER1 + n, k)

            def finish(n, half, k, slot, s_x, trip):
                dve.wait_ge(s_mm, n + 3)
                dve.wait_ge(s_store[k % 2], 16 * (half + 1))
                nc.vector.scalar_tensor_tensor(out=obuf[k % 2], in0=ps_out[k % 2], scalar=w_sum[:, 0:1],
                                               in1=row_fb, op0=ALU.mult, op1=ALU.mult).then_inc(s_scaled, 1)
                dve.wait_ge(s_x, 16 * (trip + 1))
                dve.wait_ge(s_scaled, n + 3)
                nc.vector.scalar_tensor_tensor(out=obuf[k % 2], in0=obuf[k % 2], scalar=bias_sb[:, 0:1],
                                               in1=xring[:, slot, :], op0=ALU.add, op1=ALU.add).then_inc(s_out, 1)

            def finish_res(i, k):
                finish(NR * i + k, (NR // 2) * i + k // 2, k, NO + k, s_xr[k], i)

            def finish_rest(i, k):
                finish(ORDER1 + NO * i + k, ORDER1 // 2 + (NO // 2) * i + k // 2, k, k, s_xo[k], i)

            y_res(0, 0)
            dve.wait_ge(s_dchain, 10)
            diagonal(row_f, 1.0).then_inc(s_diagf, 1)
            dve.wait_ge(s_rowp, 1)
            nc.vector.tensor_copy(row_fb, ps_rowf).then_inc(s_rowf, 1)
            dve.wait_ge(s_rowf, 1)
            with dve.Fori(0, TRIPS - 1) as i:
                for k in range(NR):
                    y_res(NR * i + k + 1, k + 1)
                    finish_res(i, k)
            for k in range(NR):
                if k < NR - 1:
                    y_res(NR * (TRIPS - 1) + k + 1, k + 1)
                else:
                    y_rest(0, 0)
                finish_res(TRIPS - 1, k)
            with dve.Fori(0, TRIPS - 1) as i:
                for k in range(NO):
                    y_rest(NO * i + k + 1, k + 1)
                    finish_rest(i, k)
            for k in range(NO):
                if k < NO - 1:
                    y_rest(NO * (TRIPS - 1) + k + 1, k + 1)
                finish_rest(TRIPS - 1, k)


_INS = ["x", "adj", "L0_gnn_bias", "L0_gnn_gumbel"]
_OUTS = [((64, 128, 1024), "float32")]


def kernel(**inputs):
    import numpy as _np
    import concourse.bacc as _bacc
    from concourse import mybir as _mybir
    from concourse.bass_utils import run_bass_kernel_spmd as _run

    nc = _bacc.Bacc("TRN2", target_bir_lowering=False, num_devices=1)
    arrays, args = {}, []
    for name in _INS:
        a = _np.ascontiguousarray(inputs[name])
        arrays[f"in_{name}_dram"] = a
        args.append(nc.dram_tensor(f"in_{name}_dram", a.shape, _mybir.dt.from_np(a.dtype), kind="ExternalInput").ap())
    for i, (shape, dtype) in enumerate(_OUTS):
        dt = _mybir.dt.from_np(_np.dtype(dtype))
        args.append(nc.dram_tensor(f"out_{i}_dram", shape, dt, kind="ExternalOutput").ap())
    gnn_kernel(nc, *args)
    r = _run(nc, [arrays], core_ids=[0])
    got = tuple(r.results[0][f"out_{i}_dram"] for i in range(len(_OUTS)))
    return got[0]
```

```python
from contextlib import ExitStack

import concourse.bass as bass
from concourse import mybir

ALU = mybir.AluOpType
ACT = mybir.ActivationFunctionType
AX_X = mybir.AxisListType.X
F32 = mybir.dt.float32
F16 = mybir.dt.float16
BF16 = mybir.dt.bfloat16

P = 128
BODY = 8
RESIDENT = 0
POOL_SUMS = (2, 5)
EPS = 1e-5
NORM_MIN = 1e-12
TINY = 1e-30
COMMON_SCALE = 0.125
W_SCALE = 1024.0
Y_SCALE = 256.0



def gnn_kernel(nc, x, adj, bias, gumbel, out):
    B, T, N = x.shape
    C = N // P
    H = 512
    TRIPS = B // BODY
    HALF = BODY // 2
    PAIRS = BODY // 2
    HC = C // 2
    NP, NT = len(POOL_SUMS), BODY - len(POOL_SUMS)
    TENSOR_SUMS = tuple(j for j in range(BODY) if j not in POOL_SUMS)
    assert T == P and N == 2 * H and B % BODY == 0 and PAIRS % 2 == 0 and RESIDENT == 0

    gumbel_rows = gumbel.rearrange("(c p d) g -> c p (d g)", p=P, d=N)
    bias_col = bias.rearrange("(t o) -> t o", o=1)

    with ExitStack() as ctx:
        def sb(name, shape, dt=F32):
            return ctx.enter_context(nc.sbuf_tensor(name, shape, dt))

        def sem(name):
            return ctx.enter_context(nc.semaphore(name))

        xring = sb("xring", [P, BODY, N])
        hring = sb("hring", [P, 4, N])
        ybuf = sb("ybuf", [P, 7, N])
        zbuf = sb("zbuf", [P, 4, N])
        obuf = sb("obuf", [P, 4, N])
        a16 = sb("a16", [P, 2, 7, HC, H], F16)
        p5 = sb("p5", [P, H])
        xw_res = sb("xw_res", [P, TRIPS, N])
        ident = sb("ident", [P, P])
        ident16 = sb("ident16", [P, P], BF16)
        ones = sb("ones", [P, P])
        ones16 = sb("ones16", [P, 1], F16)
        zeros = sb("zeros", [P, P])
        w = sb("w", [P, P])
        w_abs = sb("w_abs", [P, P])
        w_inv = sb("w_inv", [P, P])
        w_unit = sb("w_unit", [P, P])
        w16 = sb("w16", [P, 2, P], F16)
        w_sum = sb("w_sum", [P, 1])
        bias_sb = sb("bias_sb", [P, 1])
        stats = sb("stats", [P, 4, 12])
        moments = sb("moments", [P, BODY, 2])
        var_eps = sb("var_eps", [P, 2])
        neg_mean = sb("neg_mean", [P, 2])
        eps = sb("eps", [P, 2])
        minus_one = sb("minus_one", [P, 2])
        neg_half = sb("neg_half", [P, C])
        rstd = sb("rstd", [P, B])
        nbias = sb("nbias", [P, B])
        norm2 = sb("norm2", [P, C])
        rnorm = sb("rnorm", [P, C])
        degree = sb("degree", [P, C])
        has_deg = sb("has_deg", [P, C])
        dinv_raw = sb("dinv_raw", [P, C])
        dinv = sb("dinv", [P, C])
        u = sb("u", [P, C])
        row_f = sb("row_f", [P, C])
        row_count = sb("row_count", [P, C])
        col2 = sb("col2", [P, 2])
        top = sb("top", [1, 2])
        top_b = sb("top_b", [P, 2])
        small = sb("small", [P, 4])

        adjm = xring[:, 0:4, :].bitcast(BF16).rearrange("p a (b n) -> p (a b) n", b=2)
        nmask = xring[:, 4:8, :].bitcast(BF16).rearrange("p a (b n) -> p (a b) n", b=2)
        S, sq, diag, xn = (hring[:, k, :] for k in range(4))
        gum = a16[:, :, :, :, :].bitcast(F32).rearrange("p k m c n -> p (k m c n)")[:, 0:8 * N].rearrange(
            "p (r n) -> p r n", r=4)
        acc = zbuf[:, 0, :]
        sim_s = [ybuf[:, k, :] for k in (0, 1)]
        score0 = [ybuf[:, k, :] for k in (2, 3)]
        nscore1 = [ybuf[:, k, :] for k in (4, 5)]
        com2 = [ybuf[:, k, :] for k in (0, 1)]
        cmask = [ybuf[:, 2, :].bitcast(BF16)[:, k * N:(k + 1) * N] for k in (0, 1)]
        a32 = zbuf
        t32 = obuf[:, 0:2, :].rearrange("p a (b n) -> p (a b) n", b=2)
        z = zbuf[:, :, :].rearrange("p a (b n) -> p (a b) n", b=2)
        y16 = ybuf[:, :, :].bitcast(F16).rearrange("p a n -> p (a n)").rearrange(
            "p (q k u n) -> p q k u n", q=2, k=2, u=7)
        h32 = hring[:, 2, :]
        diag_f = obuf[:, 3, :]
        row_fb = hring[:, 3, :]
        h16 = [hring[:, k, :].bitcast(F16).rearrange("p (k n) -> p k n", k=2) for k in (0, 1)]
        o = [[obuf[:, 2 * q + b, :] for b in (0, 1)] for q in (0, 1)]

        ps = ctx.enter_context(nc.psum_tensor("ps", [P, 8, H], F32))
        pair = [ps[:, 2 * k:2 * k + 2, :].rearrange("p a n -> p (a n)") for k in range(4)]
        ps_avg = pair[0]
        ps_xw1 = pair[1]
        ps_w = ps[:, 7, :]
        ps_norm = ps[:, 6, 0:C]
        ps_bc = pair[1]
        ps_sim = [pair[2], pair[0]]
        ps_sym = [pair[1], pair[3]]
        ps_com = [pair[2], pair[0]]
        ps_deg = ps[:, 2, 0:C]
        ps_top = ps[:, 3, :]
        ps_rowf = pair[3]
        ps_a, ps_b, ps_d = ([ps[:, 3 * q + k, :] for q in (0, 1)] for k in range(3))
        ps_xw2 = pair[3]

        s_consts = sem("consts_loaded")
        s_x1 = [sem(f"x1_loaded{j}") for j in range(BODY)]
        s_gum = [sem(f"gumbel_loaded{k}") for k in range(4)]
        s_x2 = [sem(f"x2_loaded{j}") for j in range(BODY)]
        s_store = [sem(f"stored{k}") for k in range(4)]
        s_ident = sem("ident_built")
        s_wabs = sem("w_abs_ready")
        s_wsum = sem("w_sums_ready")
        s_w = sem("w_unit_ready")
        s_wchain = sem("w_chain")
        s_bn = sem("bn_stats_done")
        s_bnseen = sem("bn_stats_seen")
        s_mom = sem("moments_ready")
        s_pchain = sem("pool_chain")
        s_norm = sem("norms_ready")
        s_h = sem("h_ready")
        s_hpe = sem("h_summed_by_tensor")
        s_hpool = sem("h_summed_by_pool")
        s_xw1 = sem("xw1_ready")
        s_xw1used = sem("xw1_stored")
        s_S = sem("S_ready")
        s_sq = sem("sq_ready")
        s_n2 = sem("norm2_ready")
        s_n2s = sem("norm2_in_sbuf")
        s_rn = sem("rnorm_ready")
        s_diag = sem("diag_ready")
        s_bc = sem("rnorm_row_ready")
        s_xn = sem("xn_ready")
        s_sim = sem("sim_ready")
        s_sims = sem("sim_in_sbuf")
        s_sc0 = sem("score0_ready")
        s_sc1 = sem("score1_ready")
        s_adj = sem("adj_ready")
        s_sym = sem("sym_ready")
        s_mask = sem("nmask_ready")
        s_com = sem("common_ready")
        s_com2 = sem("common2_ready")
        s_cm = sem("cmask_ready")
        s_a32 = sem("a32_ready")
        s_ts = sem("t_ready")
        s_ahi = sem("a_high_ready")
        s_alo = sem("a_low_ready")
        s_dsum = sem("chunk_summed")
        s_dchain = sem("degree_chain")
        s_pow = sem("dinv_raw_ready")
        s_colmax = sem("column_maxima_ready")
        s_topT = sem("maxima_transposed")
        s_top = sem("top_ready")
        s_topb = sem("top_broadcast")
        s_u = sem("u_ready")
        s_diagf = sem("row_factor_diag_ready")
        s_rowp = sem("row_factor_in_psum")
        s_rowf = sem("row_factor_ready")
        s_h32 = sem("h32_ready")
        s_hhi = sem("h_high_ready")
        s_hlo = sem("h_low_ready")
        s_xw2 = sem("xw2_ready")
        s_z = sem("z_ready")
        s_zs = sem("z_sums_ready")
        s_yhi = sem("y_high_ready")
        s_y = sem("y_ready")
        s_mm = sem("product_ready")
        s_v = sem("partial_sum_read")
        s_c = sem("block_read")
        s_c22 = sem("c22_ready")
        s_scaled = sem("result_scaled")
        s_out = sem("out_ready")

        block = ctx.enter_context(nc.Block())
        CHUNKS = [c + HC * k for c in range(HC) for k in (0, 1)]
        GROUPS = ((0, 2), (2, 1), (3, 2), (5, 2))

        @block.sync
        def _(sp):
            for q in s_store:
                sp.sem_inc(q, 16)
            sp.dma_start(w[:], adj).then_inc(s_consts, 16)
            sp.dma_start(bias_sb[:], bias_col).then_inc(s_consts, 16)
            for j in range(BODY):
                sp.dma_start(xring[:, j, :], x[j]).then_inc(s_x1[j], 16)
            with sp.Fori(1, TRIPS) as i:
                for j in range(BODY):
                    sp.wait_ge(s_h, BODY * (i - 1) + j + 1)
                    sp.dma_start(xring[:, j, :], x[BODY * i + j]).then_inc(s_x1[j], 16)
            for c in range(C):
                if c >= 4:
                    sp.wait_ge(s_adj, c - 3)
                sp.dma_start(gum[:, c % 4, :], gumbel_rows[c]).then_inc(s_gum[c % 4], 16)

            sp.wait_ge(s_com, C)
            sp.wait_ge(s_cm, C)
            for j in range(BODY):
                sp.dma_start(xring[:, j, :], x[j]).then_inc(s_x2[j], 16)

            def store_and_reload(i, j, more):
                sp.wait_ge(s_out, BODY * i + j + 1)
                sp.dma_start(out[BODY * i + j], o[j // 2 % 2][j % 2]).then_inc(s_store[j % 4], 16)
                if more:
                    sp.dma_start(xring[:, j, :], x[BODY * (i + 1) + j]).then_inc(s_x2[j], 16)

            with sp.Fori(0, TRIPS - 1) as i:
                for j in range(BODY):
                    store_and_reload(i, j, True)
            for j in range(BODY):
                store_and_reload(TRIPS - 1, j, False)
            for q in s_store:
                sp.wait_ge(q, 16 * (B // 4 + 1))

        @block.gpsimd
        def _(pool):
            nc.gpsimd.memset(neg_half[:], -0.5).then_inc(s_pchain, 1)
            nc.gpsimd.memset(eps[:], EPS).then_inc(s_pchain, 1)
            nc.gpsimd.memset(minus_one[:], -1.0).then_inc(s_pchain, 1)
            nc.gpsimd.memset(acc, 0.0).then_inc(s_pchain, 1)
            nc.gpsimd.memset(ones16[:], 1.0).then_inc(s_pchain, 1)
            nc.gpsimd.memset(ones[:], 1.0).then_inc(s_pchain, 1)
            pool.wait_ge(s_pchain, 6)
            nc.gpsimd.affine_select(out=ident[:], in_=ones[:], compare_op=ALU.is_equal, fill=0.0, base=0,
                                    pattern=[[-1, P]], channel_multiplier=1).then_inc(s_ident, 1)
            pool.wait_ge(s_ident, 1)
            nc.gpsimd.tensor_copy(ident16[:], ident[:]).then_inc(s_ident, 1)

            def norms(i, q):
                done = 6 + 3 * (HALF * i + q)
                pool.wait_ge(s_mom, BODY * i + 2 * q + 2)
                nc.gpsimd.tensor_tensor(var_eps[:], moments[:, 2 * q:2 * q + 2, 1], eps[:],
                                        ALU.add).then_inc(s_pchain, 1)
                nc.gpsimd.tensor_tensor(neg_mean[:], moments[:, 2 * q:2 * q + 2, 0], minus_one[:],
                                        ALU.mult).then_inc(s_pchain, 1)
                pool.wait_ge(s_pchain, done + 2)
                r = rstd[:, bass.ds(BODY * i + 2 * q, 2)]
                nc.gpsimd.tensor_tensor(r, var_eps[:], neg_half[:, 0:2], ALU.pow).then_inc(s_pchain, 1)
                pool.wait_ge(s_pchain, done + 3)
                nc.gpsimd.tensor_tensor(nbias[:, bass.ds(BODY * i + 2 * q, 2)], neg_mean[:], r,
                                        ALU.mult).then_inc(s_norm, 1)
                pool.wait_ge(s_norm, HALF * (i + 1) + q + 1)

            def add(i, j):
                k = POOL_SUMS.index(j)
                pool.wait_ge(s_h, BODY * i + j + 1)
                pool.wait_ge(s_hpool, NP * (i + 1) + k)
                nc.gpsimd.tensor_tensor(acc, acc, hring[:, j % 4, :], ALU.add).then_inc(s_hpool, 1)

            pool.sem_inc(s_hpool, NP)
            pool.sem_inc(s_norm, HALF)
            with pool.Fori(0, TRIPS) as i:
                norms(i, 0)
                norms(i, 1)
                for j in range(BODY):
                    if j in POOL_SUMS:
                        add(i, j)
                    if j % 2 == 1 and j // 2 + 2 < HALF:
                        norms(i, j // 2 + 2)

            pool.wait_ge(s_n2s, 1)
            nc.gpsimd.tensor_tensor(rnorm[:], norm2[:], neg_half[:], ALU.pow).then_inc(s_rn, 1)
            for c in range(C):
                pool.wait_ge(s_sims, c + 1)
                pool.wait_ge(s_gum[c % 4], 16 * (c // 4 + 1))
                if c >= 2:
                    pool.wait_ge(s_adj, c - 1)
                nc.gpsimd.tensor_tensor(score0[c % 2], sim_s[c % 2],
                                        gum[:, c % 4, :].rearrange("p (d g) -> p g d", g=2)[:, 0, :],
                                        ALU.add).then_inc(s_sc0, 1)
            for e in range(C):
                pool.wait_ge(s_cm, e + 1)
                pool.wait_ge(s_com2, e + 1)
                if e >= 4:
                    pool.wait_ge(s_alo, 3 * (e // 2 - 1))
                    pool.wait_ge(s_dsum, e - 3)
                nc.gpsimd.tensor_tensor(a32[:, e % 4, :], com2[e % 2], cmask[e % 2], ALU.mult).then_inc(s_a32, 1)
            pool.wait_ge(s_dchain, 4)
            nc.gpsimd.tensor_tensor(dinv_raw[:], degree[:], neg_half[:], ALU.pow).then_inc(s_pow, 1)

            with pool.Fori(0, TRIPS * PAIRS) as r:
                pool.wait_ge(s_z, 2 * r + 2)
                pool.wait_ge(s_y, 4 * r + 4)
                nc.gpsimd.tensor_tensor(z[:, 4, :], z[:, 0, :], z[:, 3, :], ALU.add).then_inc(s_zs, 1)
                pool.wait_ge(s_zs, 4 * r + 1)
                nc.gpsimd.tensor_tensor(z[:, 5, :], z[:, 4, :], z[:, 1, :], ALU.subtract).then_inc(s_zs, 1)
                nc.gpsimd.tensor_tensor(z[:, 6, :], z[:, 1, :], z[:, 0, :], ALU.subtract).then_inc(s_zs, 1)
                pool.wait_ge(s_zs, 4 * r + 2)
                nc.gpsimd.tensor_tensor(z[:, 7, :], z[:, 2, :], z[:, 5, :], ALU.subtract).then_inc(s_zs, 1)

        @block.scalar
        def _(act):
            def relu1(i, j):
                act.wait_ge(s_norm, HALF * (i + 1) + j // 2 + 1)
                last = (j + 4) % BODY
                trip = i + 1 if j >= 4 else i
                if last in POOL_SUMS:
                    act.wait_ge(s_hpool, NP * trip + POOL_SUMS.index(last) + 1)
                else:
                    act.wait_ge(s_hpe, NT * trip + TENSOR_SUMS.index(last) + 1)
                t = BODY * i + j
                nc.scalar.activation(hring[:, j % 4, :], xring[:, j, :], ACT.Relu, bias=nbias[:, bass.ds(t, 1)],
                                     scale=rstd[:, bass.ds(t, 1)]).then_inc(s_h, 1)

            def keep(i):
                act.wait_ge(s_xw1, i + 1)
                nc.scalar.activation(xw_res[:, bass.ds(i, 1), :].rearrange("p a n -> p (a n)"),
                                     ps_xw1, ACT.Copy).then_inc(s_xw1used, 1)

            act.sem_inc(s_xw1used, 1)
            with act.Fori(0, TRIPS) as i:
                for j in range(BODY):
                    relu1(i, j)
                    if j == RESIDENT + 1:
                        keep(i)

            act.wait_ge(s_S, 1)
            nc.scalar.activation(sq, S, ACT.Square, scale=1.0 / B).then_inc(s_sq, 1)
            for c in range(C):
                act.wait_ge(s_sim, c + 1)
                if c >= 2:
                    act.wait_ge(s_sc0, c - 1)
                    act.wait_ge(s_sc1, c - 1)
                nc.scalar.activation(sim_s[c % 2], ps_sim[c % 2], ACT.Copy, bias=0.5,
                                     scale=0.5).then_inc(s_sims, 1)
            for c in range(C):
                act.wait_ge(s_sym, c + 1)
                nc.scalar.activation(nmask[:, c, :], ps_sym[c % 2], ACT.Sign,
                                     accum_out=row_count[:, c:c + 1]).then_inc(s_mask, 1)

            def high(e):
                c, pair = e // 2, 2 * (e // 2 % 2)
                act.wait_ge(s_a32, e + 1)
                nc.scalar.activation(a16[:, 0, 0, c, :], a32[:, pair, 0:H], ACT.Copy).then_inc(s_ahi, 1)
                nc.scalar.activation(a16[:, 0, 1:3, c, :], a32[:, pair + 1, :].rearrange("p (a n) -> p a n", a=2),
                                     ACT.Copy).then_inc(s_ahi, 1)
                act.wait_ge(s_ts, 4 * (c + 1))
                nc.scalar.activation(a16[:, 0, 3:7, c, :], t32, ACT.Copy).then_inc(s_ahi, 1)

            for e in range(C):
                act.wait_ge(s_com, e + 1)
                if e >= 2:
                    act.wait_ge(s_a32, e - 1)
                nc.scalar.activation(com2[e % 2], ps_com[e % 2], ACT.Square,
                                     scale=COMMON_SCALE).then_inc(s_com2, 1)
                if e >= 2 and e % 2 == 0:
                    high(e - 1)
            high(C - 1)

            def relu2(i, q, b):
                i, q = i + q // PAIRS, q % PAIRS
                j = 2 * q + b
                if j == RESIDENT:
                    return
                n = (BODY - 1) * i + j - 1
                act.wait_ge(s_x2[j], 16 * (i + 1))
                act.wait_ge(s_hlo, n + 1)
                back = (3 if q == 1 else 2) if b == 0 else (1 if q == 0 else 2)
                act.wait_ge(s_xw2, n + 3 - back)
                t = BODY * i + j
                bias, scale = nbias[:, bass.ds(t, 1)], rstd[:, bass.ds(t, 1)]
                nc.scalar.activation(h32, xring[:, j, :], ACT.Relu, bias=bias, scale=scale).then_inc(s_h32, 1)
                nc.scalar.activation(h16[b][:, 0, :], xring[:, j, :], ACT.Relu, bias=bias,
                                     scale=scale).then_inc(s_hhi, 1)

            def y_high(i, q, g):
                i, q = i + q // PAIRS, q % PAIRS
                r = PAIRS * i + q
                if g == 0:
                    act.wait_ge(s_z, 2 * r + 1)
                    act.wait_ge(s_mm, 7 * (r + 1))
                elif g == 1:
                    act.wait_ge(s_z, 2 * r + 2)
                else:
                    act.wait_ge(s_zs, 4 * r + 2 * g - 2)
                a, n = GROUPS[g]
                nc.scalar.activation(y16[:, q % 2, 0, a:a + n, :], z[:, a + 1:a + 1 + n, :],
                                     ACT.Copy).then_inc(s_yhi, 1)

            def partial(i, q, k):
                r = PAIRS * i + q
                if k == 0:
                    act.wait_ge(s_store[2 * (q % 2)], 16 * ((PAIRS // 2) * i + q // 2 + 1))
                    act.wait_ge(s_store[2 * (q % 2) + 1], 16 * ((PAIRS // 2) * i + q // 2 + 1))
                if k == 1:
                    act.wait_ge(s_c22, r + 1)
                act.wait_ge(s_mm, 14 + 7 * r + (1, 2, 3, 5)[k])
                dst = (o[q % 2][0][:, 0:H], p5[:], o[q % 2][0][:, H:N], o[q % 2][1][:, H:N])[k]
                src = (ps_b, ps_d, ps_b, ps_b)[k][q % 2]
                nc.scalar.activation(dst, src, ACT.Copy).then_inc(s_v, 1)

            def act_pair(i, q, ahead1, ahead2):
                partial(i, q, 0)
                if ahead1:
                    y_high(i, q + 1, 0)
                partial(i, q, 1)
                if ahead2:
                    relu2(i, q + 2, 0)
                partial(i, q, 2)
                if ahead1:
                    y_high(i, q + 1, 1)
                if ahead2:
                    relu2(i, q + 2, 1)
                if ahead1:
                    y_high(i, q + 1, 2)
                partial(i, q, 3)
                if ahead1:
                    y_high(i, q + 1, 3)

            relu2(0, 0, 1)
            y_high(0, 0, 0)
            y_high(0, 0, 1)
            relu2(0, 1, 0)
            y_high(0, 0, 2)
            y_high(0, 0, 3)
            relu2(0, 1, 1)
            with act.Fori(0, TRIPS - 1) as i:
                for q in range(PAIRS):
                    act_pair(i, q, True, True)
            for q in range(PAIRS):
                act_pair(TRIPS - 1, q, q + 1 < PAIRS, q + 2 < PAIRS)

        @block.tensor
        def _(pe):
            pe.sem_inc(s_hpe, NT)
            pe.sem_inc(s_mm, 14)
            pe.sem_inc(s_xw2, 2)
            pe.wait_ge(s_wabs, 1)
            pe.wait_ge(s_ident, 2)
            nc.tensor.matmul(ps_w[:, 0:P], ones[:], w_abs[:], start=True, stop=True)
            nc.tensor.matmul(ps_w[:, P:P + 1], w_abs[:], ones[:, 0:1], start=True, stop=True,
                             skip_group_check=True).then_inc(s_wsum, 1)
            for m in range(2):
                nc.tensor.matmul(ps_avg[:, m * H:m * H + P], zeros[:], ones[:], start=True, stop=True,
                                 skip_group_check=True)

            def bcast(dst, src):
                for m in range(2):
                    mm = nc.tensor.matmul(dst[:, m * H:(m + 1) * H], ones[:], src[:, m * H:(m + 1) * H],
                                          start=True, stop=True)
                return mm

            pe.wait_ge(s_w, 1)
            with pe.Fori(0, TRIPS) as i:
                for j in range(BODY):
                    h = hring[:, j % 4, :]
                    if j == RESIDENT:
                        pe.wait_ge(s_h, BODY * i + j + 1)
                        pe.wait_ge(s_xw1used, i + 1)
                        for c in range(C):
                            mm = nc.tensor.matmul(ps_xw1[:, c * P:(c + 1) * P], h[:, c * P:(c + 1) * P], w_unit[:],
                                                  start=True, stop=True, skip_group_check=True)
                        mm.then_inc(s_xw1, 1)
                    if j in TENSOR_SUMS:
                        pe.wait_ge(s_h, BODY * i + j + 1)
                        for m in range(2):
                            mm = nc.tensor.matmul(ps_avg[:, m * H:(m + 1) * H], ident[:], h[:, m * H:(m + 1) * H],
                                                  start=False, stop=True, skip_group_check=True)
                        mm.then_inc(s_hpe, 1)

            pe.wait_ge(s_sq, 1)
            for c in range(C):
                mm = nc.tensor.matmul(ps_norm[:, c:c + 1], sq[:, c * P:(c + 1) * P], ones[:, 0:1],
                                      start=True, stop=True, skip_group_check=True)
            mm.then_inc(s_n2, 1)
            pe.wait_ge(s_diag, 1)
            bcast(ps_bc, diag).then_inc(s_bc, 1)
            pe.wait_ge(s_xn, 1)
            for c in range(C):
                if c >= 2:
                    pe.wait_ge(s_sims, c - 1)
                for m in range(2):
                    mm = nc.tensor.matmul(ps_sim[c % 2][:, m * H:(m + 1) * H], xn[:, c * P:(c + 1) * P],
                                          xn[:, m * H:(m + 1) * H], start=True, stop=True)
                mm.then_inc(s_sim, 1)
            pe.wait_ge(s_adj, C)
            for c in range(C):
                if c >= 2:
                    pe.wait_ge(s_mask, c - 1)
                for m in range(2):
                    nc.tensor.matmul(ps_sym[c % 2][:, m * H:(m + 1) * H], ident16[:], adjm[:, c, m * H:(m + 1) * H],
                                     start=True, stop=False, skip_group_check=True)
                for k in range(C):
                    nc.tensor.matmul(ps_sym[c % 2][:, k * P:(k + 1) * P], adjm[:, k, c * P:(c + 1) * P], ident16[:],
                                     start=False, stop=k != c, skip_group_check=True)
                nc.tensor.matmul(ps_sym[c % 2][:, c * P:(c + 1) * P], ident16[:], ident16[:],
                                 start=False, stop=True, skip_group_check=True).then_inc(s_sym, 1)

            def degrees(e):
                pe.wait_ge(s_a32, e + 1)
                for d in range(C):
                    mm = nc.tensor.matmul(ps_deg[:, d:d + 1], a32[:, e % 4, d * P:(d + 1) * P], ones[:, 0:1],
                                          start=(e == d == 0), stop=(e == C - 1), skip_group_check=True)
                mm.then_inc(s_dsum, 1)

            def spread(col, s_in, n, s_done):
                pe.wait_ge(s_in, n + 1)
                nc.tensor.transpose(ps_top[0:1, 0:P], col, ident[:]).then_inc(s_done, 1)
                pe.wait_ge(s_top, n + 1)
                nc.tensor.matmul(ps_top[:, P:P + 1], ones[0:1, :], top[:, n:n + 1], start=True, stop=True,
                                 skip_group_check=True).then_inc(s_topb, 1)

            pe.wait_ge(s_mask, C)
            for e, c in enumerate(CHUNKS):
                if e >= 2:
                    pe.wait_ge(s_com2, e - 1)
                for k in range(C):
                    for m in range(2):
                        mm = nc.tensor.matmul(ps_com[e % 2][:, m * H:(m + 1) * H], nmask[:, k, c * P:(c + 1) * P],
                                              nmask[:, k, m * H:(m + 1) * H], start=(k == 0), stop=(k == C - 1))
                mm.then_inc(s_com, 1)
                if e == 1:
                    spread(col2[:, 0:1], s_colmax, 0, s_topT)
                if e >= 2:
                    degrees(e - 2)
            degrees(C - 2)
            degrees(C - 1)
            spread(col2[:, 1:2], s_colmax, 1, s_topT)

            def xw_of(i, q, b):
                i, q = i + q // PAIRS, q % PAIRS
                j = 2 * q + b
                if j == RESIDENT:
                    return
                pe.wait_ge(s_hlo, (BODY - 1) * i + j + 1)
                pe.wait_ge(s_z, BODY * i + j)
                for c in range(C):
                    for hk, wk in ((0, 0), (0, 1), (1, 0)):
                        mm = nc.tensor.matmul(ps_xw2[:, c * P:(c + 1) * P], h16[b][:, hk, c * P:(c + 1) * P],
                                              w16[:, wk, :], start=(hk == wk == 0), stop=(hk == 1),
                                              skip_group_check=True)
                mm.then_inc(s_xw2, 1)

            def product(q, u, mat, bank, start):
                for c in range(HC):
                    for yk, ak in ((0, 0), (0, 1), (1, 0)):
                        mm = nc.tensor.matmul(bank[q % 2], y16[:, q % 2, yk, u, c * P:(c + 1) * P],
                                              a16[:, ak, mat, c, :], start=(start and c == yk == ak == 0),
                                              stop=(c == HC - 1 and yk == 1), skip_group_check=True)
                mm.then_inc(s_mm, 1)

            def pe_pair(i, q, ahead1):
                r = PAIRS * i + q
                pe.wait_ge(s_y, 4 * r + 5)
                pe.wait_ge(s_c, 3 * r + 3)
                product(q, 0, 0, ps_b, True)
                if ahead1:
                    xw_of(i, q + 1, 0)
                pe.wait_ge(s_y, 4 * r + 7)
                product(q, 3, 3, ps_d, True)
                pe.wait_ge(s_v, 4 * r + 1)
                product(q, 4, 4, ps_b, False)
                if ahead1:
                    xw_of(i, q + 1, 1)
                pe.wait_ge(s_y, 4 * r + 8)
                pe.wait_ge(s_v, 4 * r + 2)
                product(q, 6, 2, ps_d, False)
                pe.wait_ge(s_v, 4 * r + 3)
                product(q, 5, 5, ps_b, False)
                product(q, 1, 1, ps_a, True)
                pe.wait_ge(s_v, 4 * r + 4)
                product(q, 2, 6, ps_b, False)

            pe.wait_ge(s_diagf, 1)
            bcast(ps_rowf, diag_f).then_inc(s_rowp, 1)
            pe.wait_ge(s_rowf, 1)
            xw_of(0, 0, 1)
            with pe.Fori(0, TRIPS - 1) as i:
                for q in range(PAIRS):
                    pe_pair(i, q, True)
            for q in range(PAIRS):
                pe_pair(TRIPS - 1, q, q + 1 < PAIRS)

        @block.vector
        def _(dve):
            dve.sem_inc(s_c, 6)
            dve.sem_inc(s_y, 4)
            dve.sem_inc(s_hlo, 1)
            dve.sem_inc(s_c22, 1)
            nc.vector.memset(zeros[:], 0.0).then_inc(s_wchain, 1)
            dve.wait_ge(s_consts, 32)
            nc.vector.scalar_tensor_tensor(out=w_abs[:], in0=w[:], scalar=-1.0, in1=w[:], op0=ALU.mult,
                                           op1=ALU.max).then_inc(s_wabs, 1)
            dve.wait_ge(s_wsum, 1)
            nc.vector.tensor_scalar(w_inv[:], ps_w[:, 0:P], TINY, None, ALU.max).then_inc(s_wchain, 1)
            nc.vector.tensor_scalar(w_sum[:], ps_w[:, P:P + 1], TINY, None, ALU.max).then_inc(s_wchain, 1)
            dve.wait_ge(s_wchain, 3)
            nc.vector.reciprocal(w_unit[:], w_inv[:]).then_inc(s_wchain, 1)
            dve.wait_ge(s_wchain, 4)
            nc.vector.scalar_tensor_tensor(out=w_inv[:], in0=w_unit[:], scalar=W_SCALE, in1=w[:], op0=ALU.mult,
                                           op1=ALU.mult).then_inc(s_wchain, 1)
            dve.wait_ge(s_wchain, 5)
            nc.vector.tensor_copy(w_unit[:], w_inv[:]).then_inc(s_w, 1)
            nc.vector.tensor_copy(w16[:, 0, :], w_inv[:]).then_inc(s_wchain, 1)
            dve.wait_ge(s_wchain, 6)
            nc.vector.tensor_tensor(w16[:, 1, :], w_inv[:], w16[:, 0, :], ALU.subtract).then_inc(s_wchain, 1)

            with dve.Fori(0, TRIPS) as i:
                for q in range(HALF):
                    for j in (2 * q, 2 * q + 1):
                        dve.wait_ge(s_x1[j], 16 * (i + 1))
                        for m in range(2):
                            nc.vector.bn_stats(stats[:, j % 4, 6 * m:6 * m + 6],
                                               xring[:, j, m * H:(m + 1) * H]).then_inc(s_bn, 1)
                    dve.wait_ge(s_norm, HALF * i + q + 1)
                    dve.wait_ge(s_bn, 4 * (HALF * i + q) + 4)
                    dve.sem_inc(s_bnseen, 1)
                    for j in (2 * q, 2 * q + 1):
                        nc.vector.bn_aggr(moments[:, j, :], stats[:, j % 4, :]).then_inc(s_mom, 1)

            dve.wait_ge(s_hpe, NT * (TRIPS + 1))
            dve.wait_ge(s_hpool, NP * (TRIPS + 1))
            nc.vector.tensor_tensor(S, ps_avg, acc, ALU.add).then_inc(s_S, 1)
            dve.wait_ge(s_n2, 1)
            nc.vector.tensor_scalar(norm2[:], ps_norm, NORM_MIN ** 2, None, ALU.max).then_inc(s_n2s, 1)

            def diagonal(dst, col, factor):
                return nc.vector.scalar_tensor_tensor(
                    out=dst.rearrange("p (c n) -> p c n", c=C), in0=ident[:].unsqueeze(1).broadcast_to([P, C, P]),
                    scalar=factor, in1=col[:].unsqueeze(2).broadcast_to([P, C, P]), op0=ALU.mult, op1=ALU.mult)

            dve.wait_ge(s_rn, 1)
            diagonal(diag, rnorm, 1.0 / B).then_inc(s_diag, 1)
            dve.wait_ge(s_bc, 1)
            dve.wait_ge(s_S, 1)
            nc.vector.tensor_tensor(xn, S, ps_bc, ALU.mult).then_inc(s_xn, 1)
            for c in range(C):
                dve.wait_ge(s_sims, c + 1)
                dve.wait_ge(s_gum[c % 4], 16 * (c // 4 + 1))
                if c >= 2:
                    dve.wait_ge(s_adj, c - 1)
                nc.vector.scalar_tensor_tensor(out=nscore1[c % 2], in0=sim_s[c % 2], scalar=1.0,
                                               in1=gum[:, c % 4, :].rearrange("p (d g) -> p g d", g=2)[:, 1, :],
                                               op0=ALU.subtract, op1=ALU.subtract).then_inc(s_sc1, 1)
                dve.wait_ge(s_sc1, c + 1)
                dve.wait_ge(s_sc0, c + 1)
                nc.vector.scalar_tensor_tensor(out=adjm[:, c, :], in0=nscore1[c % 2], scalar=-1.0, in1=score0[c % 2],
                                               op0=ALU.mult, op1=ALU.is_lt).then_inc(s_adj, 1)

            dve.wait_ge(s_mask, C)
            nc.vector.tensor_reduce(col2[:, 0:1], row_count[:], AX_X, ALU.max).then_inc(s_colmax, 1)

            def top_of(n):
                dve.wait_ge(s_topT, n + 1)
                nc.vector.tensor_reduce(top[:, n:n + 1], ps_top[0:1, 0:P], AX_X, ALU.max).then_inc(s_top, 1)

            def ts(e):
                c, k = e // 2, 2 * (e // 2 % 2)
                dve.wait_ge(s_a32, e + 1)
                if c >= 1:
                    dve.wait_ge(s_alo, 3 * c)
                a11, a12 = a32[:, k, 0:H], a32[:, k, H:N]
                a21, a22 = a32[:, k + 1, 0:H], a32[:, k + 1, H:N]
                nc.vector.tensor_tensor(t32[:, 0, :], a12, a11, ALU.subtract).then_inc(s_ts, 1)
                nc.vector.tensor_tensor(t32[:, 2, :], a22, a12, ALU.subtract).then_inc(s_ts, 1)
                dve.wait_ge(s_ts, 4 * c + 1)
                nc.vector.tensor_tensor(t32[:, 1, :], a22, t32[:, 0, :], ALU.subtract).then_inc(s_ts, 1)
                dve.wait_ge(s_ts, 4 * c + 3)
                nc.vector.tensor_tensor(t32[:, 3, :], a21, t32[:, 1, :], ALU.subtract).then_inc(s_ts, 1)

            def low(e):
                c, k = e // 2, 2 * (e // 2 % 2)
                dve.wait_ge(s_ahi, 3 * c + 1)
                nc.vector.tensor_tensor(a16[:, 1, 0, c, :], a32[:, k, 0:H], a16[:, 0, 0, c, :],
                                        ALU.subtract).then_inc(s_alo, 1)
                dve.wait_ge(s_ahi, 3 * c + 2)
                nc.vector.tensor_tensor(a16[:, 1, 1:3, c, :], a32[:, k + 1, :].rearrange("p (a n) -> p a n", a=2),
                                        a16[:, 0, 1:3, c, :], ALU.subtract).then_inc(s_alo, 1)
                dve.wait_ge(s_ts, 4 * c + 4)
                dve.wait_ge(s_ahi, 3 * c + 3)
                nc.vector.tensor_tensor(a16[:, 1, 3:7, c, :], t32, a16[:, 0, 3:7, c, :],
                                        ALU.subtract).then_inc(s_alo, 1)

            for e, c in enumerate(CHUNKS):
                dve.wait_ge(s_com2, e + 1)
                if e >= 2:
                    dve.wait_ge(s_a32, e - 1)
                nc.vector.scalar_tensor_tensor(out=cmask[e % 2], in0=com2[e % 2], scalar=COMMON_SCALE ** 2,
                                               in1=adjm[:, c, :], op0=ALU.is_gt, op1=ALU.mult).then_inc(s_cm, 1)
                if e == 1:
                    top_of(0)
                    dve.wait_ge(s_topb, 1)
                    nc.vector.tensor_copy(top_b[:, 0:1], ps_top[:, P:P + 1]).then_inc(s_dchain, 1)
                if e >= 2 and e % 2 == 0:
                    ts(e - 1)
                    low(e - 1)
            ts(C - 1)
            dve.wait_ge(s_dchain, 1)
            nc.vector.reciprocal(small[:, 0:1], top_b[:, 0:1]).then_inc(s_dchain, 1)
            dve.wait_ge(s_dchain, 2)
            nc.vector.tensor_scalar(small[:, 1:2], small[:, 0:1], COMMON_SCALE ** -2, None,
                                    ALU.mult).then_inc(s_dchain, 1)
            dve.wait_ge(s_dchain, 3)
            dve.wait_ge(s_dsum, C)
            nc.vector.tensor_scalar(degree[:], ps_deg, small[:, 1:2], TINY, ALU.mult, ALU.max).then_inc(s_dchain, 1)
            nc.vector.tensor_scalar(has_deg[:], ps_deg, 0.0, None, ALU.is_gt).then_inc(s_dchain, 1)
            low(C - 1)
            dve.wait_ge(s_pow, 1)
            dve.wait_ge(s_dchain, 5)
            nc.vector.tensor_tensor(dinv[:], dinv_raw[:], has_deg[:], ALU.mult).then_inc(s_dchain, 1)
            dve.wait_ge(s_dchain, 6)
            nc.vector.tensor_reduce(col2[:, 1:2], dinv[:], AX_X, ALU.max).then_inc(s_colmax, 1)
            top_of(1)
            dve.wait_ge(s_topb, 2)
            nc.vector.tensor_scalar(top_b[:, 1:2], ps_top[:, P:P + 1], TINY, None, ALU.max).then_inc(s_dchain, 1)
            dve.wait_ge(s_dchain, 7)
            nc.vector.reciprocal(small[:, 2:3], top_b[:, 1:2]).then_inc(s_dchain, 1)
            dve.wait_ge(s_dchain, 8)
            nc.vector.tensor_scalar(u[:], dinv[:], small[:, 2:3], Y_SCALE / W_SCALE, ALU.mult, ALU.mult).then_inc(s_u, 1)
            nc.vector.tensor_scalar(small[:, 3:4], top_b[:, 1:2], small[:, 1:2], 1.0 / Y_SCALE,
                                    ALU.mult, ALU.mult).then_inc(s_dchain, 1)
            dve.wait_ge(s_dchain, 9)
            nc.vector.tensor_scalar(row_f[:], dinv[:], small[:, 3:4], None, ALU.mult).then_inc(s_dchain, 1)
            dve.wait_ge(s_u, 1)

            def h_low(i, q, b):
                i, q = i + q // PAIRS, q % PAIRS
                j = 2 * q + b
                if j == RESIDENT:
                    return
                n = (BODY - 1) * i + j - 1
                dve.wait_ge(s_h32, n + 1)
                dve.wait_ge(s_hhi, n + 1)
                nc.vector.tensor_tensor(h16[b][:, 1, :], h32, h16[b][:, 0, :], ALU.subtract).then_inc(s_hlo, 1)

            def z_of(i, q, b):
                i, q = i + q // PAIRS, q % PAIRS
                j, r = 2 * q + b, PAIRS * i + q
                if b == 0:
                    dve.wait_ge(s_y, 4 * r + 4)
                if j == RESIDENT:
                    src = xw_res[:, bass.ds(i, 1), :].rearrange("p a (m c t) -> p (a m) c t", m=2, c=HC)
                else:
                    dve.wait_ge(s_xw2, (BODY - 1) * i + j + 2)
                    src = ps_xw2.rearrange("p (m c t) -> p m c t", m=2, c=HC)
                dst = z[:, 1:3, :] if b == 0 else z[:, 0:4:3, :]
                nc.vector.tensor_tensor(dst.rearrange("p m (c t) -> p m c t", c=HC), src,
                                        u[:].rearrange("p (m c) -> p m c", m=2).unsqueeze(3).broadcast_to(
                                            [P, 2, HC, P]), ALU.mult).then_inc(s_z, 1)

            def y_low(i, q, g):
                i, q = i + q // PAIRS, q % PAIRS
                dve.wait_ge(s_yhi, 4 * (PAIRS * i + q) + g + 1)
                a, n = GROUPS[g]
                nc.vector.tensor_tensor(y16[:, q % 2, 1, a:a + n, :], z[:, a + 1:a + 1 + n, :],
                                        y16[:, q % 2, 0, a:a + n, :], ALU.subtract).then_inc(s_y, 1)

            def scale(dst, src, cols):
                return nc.vector.scalar_tensor_tensor(out=dst, in0=src, scalar=w_sum[:, 0:1], in1=row_fb[:, cols],
                                                      op0=ALU.mult, op1=ALU.mult)

            def finish(i, q, b):
                j, ob = 2 * q + b, o[q % 2][b]
                dve.wait_ge(s_x2[j], 16 * (i + 1))
                nc.vector.scalar_tensor_tensor(out=ob, in0=ob, scalar=bias_sb[:, 0:1], in1=xring[:, j, :],
                                               op0=ALU.add, op1=ALU.add).then_inc(s_out, 1)

            LO, HI = slice(0, H), slice(H, N)

            def dve_pair(i, q, ahead1, ahead2):
                r = PAIRS * i + q
                o0, o1 = o[q % 2]
                if ahead1:
                    z_of(i, q + 1, 0)
                if ahead1:
                    y_low(i, q + 1, 0)
                if ahead2:
                    h_low(i, q + 2, 0)
                if ahead1:
                    z_of(i, q + 1, 1)
                    y_low(i, q + 1, 1)
                dve.wait_ge(s_mm, 14 + 7 * r + 4)
                dve.wait_ge(s_v, 4 * r + 3)
                nc.vector.tensor_tensor(o0[:, HI], ps_d[q % 2], o0[:, HI], ALU.add).then_inc(s_c, 1)
                if ahead2:
                    h_low(i, q + 2, 1)
                if ahead1:
                    y_low(i, q + 1, 2)
                dve.wait_ge(s_v, 4 * r + 4)
                nc.vector.tensor_tensor(o1[:, HI], o1[:, HI], p5[:], ALU.add).then_inc(s_c22, 1)
                dve.wait_ge(s_c22, r + 2)
                scale(o1[:, HI], o1[:, HI], HI).then_inc(s_scaled, 1)
                dve.wait_ge(s_mm, 14 + 7 * r + 6)
                nc.vector.tensor_tensor(o0[:, LO], ps_a[q % 2], o0[:, LO], ALU.add).then_inc(s_c, 1)
                if ahead1:
                    y_low(i, q + 1, 3)
                dve.wait_ge(s_c, 6 + 3 * r + 2)
                scale(o0, o0, slice(0, N)).then_inc(s_scaled, 1)
                dve.wait_ge(s_scaled, 2 * r + 2)
                finish(i, q, 0)
                dve.wait_ge(s_mm, 14 + 7 * r + 7)
                scale(o1[:, LO], ps_b[q % 2], LO).then_inc(s_c, 1)
                dve.wait_ge(s_c, 6 + 3 * r + 3)
                finish(i, q, 1)

            z_of(0, 0, 0)
            dve.wait_ge(s_dchain, 10)
            diagonal(diag_f, row_f, 1.0).then_inc(s_diagf, 1)
            dve.wait_ge(s_rowp, 1)
            nc.vector.tensor_copy(row_fb, ps_rowf).then_inc(s_rowf, 1)
            dve.wait_ge(s_rowf, 1)
            h_low(0, 0, 1)
            y_low(0, 0, 0)
            z_of(0, 0, 1)
            y_low(0, 0, 1)
            h_low(0, 1, 0)
            y_low(0, 0, 2)
            y_low(0, 0, 3)
            h_low(0, 1, 1)
            with dve.Fori(0, TRIPS - 1) as i:
                for q in range(PAIRS):
                    dve_pair(i, q, True, True)
            for q in range(PAIRS):
                dve_pair(TRIPS - 1, q, q + 1 < PAIRS, q + 2 < PAIRS)


_INS = ["x", "adj", "L0_gnn_bias", "L0_gnn_gumbel"]
_OUTS = [((64, 128, 1024), "float32")]


def kernel(**inputs):
    import numpy as _np
    import concourse.bacc as _bacc
    from concourse import mybir as _mybir
    from concourse.bass_utils import run_bass_kernel_spmd as _run

    nc = _bacc.Bacc("TRN2", target_bir_lowering=False, num_devices=1)
    arrays, args = {}, []
    for name in _INS:
        a = _np.ascontiguousarray(inputs[name])
        arrays[f"in_{name}_dram"] = a
        args.append(nc.dram_tensor(f"in_{name}_dram", a.shape, _mybir.dt.from_np(a.dtype), kind="ExternalInput").ap())
    for i, (shape, dtype) in enumerate(_OUTS):
        dt = _mybir.dt.from_np(_np.dtype(dtype))
        args.append(nc.dram_tensor(f"out_{i}_dram", shape, dt, kind="ExternalOutput").ap())
    gnn_kernel(nc, *args)
    r = _run(nc, [arrays], core_ids=[0])
    got = tuple(r.results[0][f"out_{i}_dram"] for i in range(len(_OUTS)))
    return got[0]
```

```python
from contextlib import ExitStack

import concourse.bass as bass
from concourse import mybir

ALU = mybir.AluOpType
ACT = mybir.ActivationFunctionType
AX_X = mybir.AxisListType.X
F32 = mybir.dt.float32
F16 = mybir.dt.float16
BF16 = mybir.dt.bfloat16

P = 128
BODY1 = 16
KEPT = (0, 8)
KEEP_AFTER = (4, 15)
POOL_SUMS = (0, 3, 6, 8, 12)
VECTOR_SUMS = (10, 12, 14)
NORM_GROUPS = ((0, 2), (2, 2), (4, 4), (8, 4), (12, 2), (14, 2))
BODY = 8
RESIDENT = 0
GUMBEL_SLOTS = 7
SUMMED = 3
EPS = 1e-5
NORM_MIN = 1e-12
TINY = 1e-30
COMMON_SCALE = 0.125
W_SCALE = 1024.0
Y_SCALE = 256.0


def gnn_kernel(nc, x, adj, bias, gumbel, out):
    B, T, N = x.shape
    C = N // P
    H = 512
    TRIPS1, TRIPS = B // BODY1, B // BODY
    NG, HS = len(NORM_GROUPS), 8
    PAIRS = BODY // 2
    HC = C // 2
    NP, NT, NK = len(POOL_SUMS), BODY1 - len(POOL_SUMS), len(KEPT)
    TENSOR_SUMS = tuple(j for j in range(BODY1) if j not in POOL_SUMS)
    assert SUMMED == C - 5
    assert T == P and N == 2 * H and B % BODY == B % BODY1 == 0
    assert NK * TRIPS1 == TRIPS and PAIRS % 2 == 0 and RESIDENT == 0

    gumbel_rows = gumbel.rearrange("(c p d) g -> c p (d g)", p=P, d=N)
    bias_col = bias.rearrange("(t o) -> t o", o=1)

    with ExitStack() as ctx:
        def sb(name, shape, dt=F32):
            return ctx.enter_context(nc.sbuf_tensor(name, shape, dt))

        def sem(name):
            return ctx.enter_context(nc.semaphore(name))

        xring = sb("xring", [P, BODY, N])
        hring = sb("hring", [P, 4, N])
        ybuf = sb("ybuf", [P, 7, N])
        zbuf = sb("zbuf", [P, 4, N])
        obuf = sb("obuf", [P, 4, N])
        a16 = sb("a16", [P, 2, 7, HC, H], F16)
        p5 = sb("p5", [P, H])
        xw_res = sb("xw_res", [P, TRIPS, N])
        ident = sb("ident", [P, P])
        ident16 = sb("ident16", [P, P], BF16)
        ones = sb("ones", [P, P])
        zeros = sb("zeros", [P, P])
        w = sb("w", [P, P])
        w_abs = sb("w_abs", [P, P])
        w_inv = sb("w_inv", [P, P])
        w_unit = sb("w_unit", [P, P])
        w16 = sb("w16", [P, 2, P], F16)
        w_sum = sb("w_sum", [P, 1])
        bias_sb = sb("bias_sb", [P, 1])
        stats = sb("stats", [P, 4, 12])
        moments = sb("moments", [P, BODY1, 2])
        var_eps = sb("var_eps", [P, 4])
        neg_mean = sb("neg_mean", [P, 4])
        eps = sb("eps", [P, 4])
        minus_one = sb("minus_one", [P, 4])
        neg_half = sb("neg_half", [P, C])
        rstd = sb("rstd", [P, B])
        nbias = sb("nbias", [P, B])
        norm2 = sb("norm2", [P, C])
        rnorm = sb("rnorm", [P, C])
        degree = sb("degree", [P, C])
        has_deg = sb("has_deg", [P, C])
        dinv_raw = sb("dinv_raw", [P, C])
        dinv = sb("dinv", [P, C])
        u = sb("u", [P, C])
        row_f = sb("row_f", [P, C])
        row_count = sb("row_count", [P, C])
        col2 = sb("col2", [P, 2])
        top = sb("top", [1, 2])
        top_b = sb("top_b", [P, 2])
        small = sb("small", [P, 4])

        adjm = xring[:, 0:4, :].bitcast(BF16).rearrange("p a (b n) -> p (a b) n", b=2)
        nmask = xring[:, 4:8, :].bitcast(BF16).rearrange("p a (b n) -> p (a b) n", b=2)
        S, sq, xn = (hring[:, k, :] for k in (0, 1, 3))
        x1 = ([xring[:, k, :] for k in range(8)] + [ybuf[:, k, :] for k in range(7)] + [obuf[:, 0, :]])
        gum = a16[:, :, :, :, :].bitcast(F32).rearrange("p k m c n -> p (k m c n)").rearrange(
            "p (r n) -> p r n", r=GUMBEL_SLOTS)
        h1 = [hring[:, k, :] for k in range(4)] + [zbuf[:, k, :] for k in (1, 2, 3)] + [obuf[:, 1, :]]
        acc = zbuf[:, 0, :]
        sim_s = [ybuf[:, k, :] for k in (0, 1)]
        score0 = [ybuf[:, k, :] for k in (2, 3)]
        nscore1 = [ybuf[:, k, :] for k in (4, 5)]
        com2 = [ybuf[:, k, :] for k in range(4)]
        cmask = [ybuf[:, 4 + k // 2, :].bitcast(BF16)[:, k % 2 * N:(k % 2 + 1) * N] for k in range(4)]
        t32 = [obuf[:, k:k + 2, :].rearrange("p a (b n) -> p (a b) n", b=2) for k in (0, 2)]
        z = zbuf[:, :, :].rearrange("p a (b n) -> p (a b) n", b=2)
        y16 = ybuf[:, :, :].bitcast(F16).rearrange("p a n -> p (a n)").rearrange(
            "p (q k u n) -> p q k u n", q=2, k=2, u=7)
        h32 = hring[:, 2, :]
        asum = zbuf[:, 3, :]
        row_fb = hring[:, 3, :]
        h16 = [hring[:, k, :].bitcast(F16).rearrange("p (k n) -> p k n", k=2) for k in (0, 1)]
        o = [[obuf[:, 2 * q + b, :] for b in (0, 1)] for q in (0, 1)]

        ps = ctx.enter_context(nc.psum_tensor("ps", [P, 8, H], F32))
        pair = [ps[:, 2 * k:2 * k + 2, :].rearrange("p a n -> p (a n)") for k in range(4)]
        ps_avg = pair[0]
        ps_xw1 = pair[1]
        ps_w = ps[:, 7, :]
        ps_norm = ps[:, 6, 0:C]
        ps_bc = pair[1]
        ps_sim = [pair[2], pair[0]]
        ps_sym = [pair[1], pair[3], pair[2], pair[0]]
        ps_com = [pair[3], pair[2], pair[0]]
        ps_deg = ps[:, 2, 0:C]
        ps_top = ps[:, 3, :]
        ps_rowf = pair[2]
        ps_a, ps_b, ps_d = ([ps[:, 3 * q + k, :] for q in (0, 1)] for k in range(3))
        ps_xw2 = pair[3]

        s_consts = sem("consts_loaded")
        s_x1 = [sem(f"x1_loaded{j}") for j in range(BODY1)]
        s_gum = [sem(f"gumbel_loaded{k}") for k in range(C)]
        s_x2 = [sem(f"x2_loaded{j}") for j in range(BODY)]
        s_store = [sem(f"stored{k}") for k in range(4)]
        s_ident = sem("ident_built")
        s_wabs = sem("w_abs_ready")
        s_wsum = sem("w_sums_ready")
        s_w = sem("w_unit_ready")
        s_wchain = sem("w_chain")
        s_bn = sem("bn_stats_done")
        s_bnseen = sem("bn_stats_seen")
        s_mom = sem("moments_ready")
        s_pchain = sem("pool_chain")
        s_norm = sem("norms_ready")
        s_h = sem("h_ready")
        s_hpe = sem("h_summed_by_tensor")
        s_hpool = sem("h_summed_by_pool")
        s_xw1 = sem("xw1_ready")
        s_xw1used = sem("xw1_stored")
        s_mine = sem("h_summed_by_vector")
        s_S = sem("S_ready")
        s_sq = sem("sq_ready")
        s_n2 = sem("norm2_ready")
        s_n2s = sem("norm2_in_sbuf")
        s_rn = sem("rnorm_ready")
        s_bc = sem("rnorm_row_ready")
        s_xn = sem("xn_ready")
        s_sim = sem("sim_ready")
        s_sims = sem("sim_in_sbuf")
        s_sc0 = sem("score0_ready")
        s_sc1 = sem("score1_ready")
        s_adj = sem("adj_ready")
        s_sym = sem("sym_ready")
        s_mask = [sem(f"nmask_ready{k}") for k in (0, 1)]
        s_com = sem("common_ready")
        s_com2 = sem("common2_ready")
        s_cm = sem("cmask_ready")
        s_a32 = sem("a32_ready")
        s_asum = sem("a_summed")
        s_ts = sem("t124_ready")
        s_t3 = sem("t3_ready")
        s_ahi = sem("a_high_ready")
        s_alo = sem("a_low_ready")
        s_dsum = sem("chunk_summed")
        s_dchain = sem("degree_chain")
        s_pow = sem("dinv_raw_ready")
        s_colmax = sem("column_maxima_ready")
        s_topT = sem("maxima_transposed")
        s_top = sem("top_ready")
        s_topb = sem("top_broadcast")
        s_u = sem("u_ready")
        s_rowp = sem("row_factor_in_psum")
        s_rowf = sem("row_factor_ready")
        s_h32 = sem("h32_ready")
        s_hhi = sem("h_high_ready")
        s_hlo = sem("h_low_ready")
        s_xw2 = sem("xw2_ready")
        s_z = sem("z_ready")
        s_zs = sem("z_sums_ready")
        s_yhi = sem("y_high_ready")
        s_y = sem("y_ready")
        s_mm = sem("product_ready")
        s_v = sem("partial_sum_read")
        s_c = sem("block_read")
        s_c22 = sem("c22_ready")
        s_scaled = sem("result_scaled")
        s_out = sem("out_ready")

        block = ctx.enter_context(nc.Block())
        def norm_group(j):
            return [a + n > j for a, n in NORM_GROUPS].index(True)

        def a32(e):
            return (hring[:, e, :] if e < 4 else zbuf[:, e - 4, :] if e < C - 1 else ybuf[:, 6, :])

        CHUNKS = [c + HC * k for c in range(HC) for k in (0, 1)]
        LO, HI = slice(0, H), slice(H, N)
        GROUPS = ((0, 2), (2, 1), (3, 2), (5, 2))

        @block.sync
        def _(sp):
            for q in s_store:
                sp.sem_inc(q, 16)
            sp.dma_start(w[:], adj).then_inc(s_consts, 16)
            sp.dma_start(bias_sb[:], bias_col).then_inc(s_consts, 16)
            for j in range(BODY1):
                sp.dma_start(x1[j], x[j]).then_inc(s_x1[j], 16)
            with sp.Fori(1, TRIPS1) as i:
                for j in range(BODY1):
                    sp.wait_ge(s_h, BODY1 * (i - 1) + j + 1)
                    sp.dma_start(x1[j], x[BODY1 * i + j]).then_inc(s_x1[j], 16)
            for c in range(C):
                if c >= GUMBEL_SLOTS:
                    sp.wait_ge(s_adj, c - GUMBEL_SLOTS + 1)
                sp.dma_start(gum[:, c % GUMBEL_SLOTS, :], gumbel_rows[c]).then_inc(s_gum[c], 16)

            sp.wait_ge(s_com, C)
            sp.wait_ge(s_cm, C)
            for j in (1, 2, 3, 0, 4, 5, 6, 7):
                sp.dma_start(xring[:, j, :], x[j]).then_inc(s_x2[j], 16)

            def store_and_reload(i, j, more):
                sp.wait_ge(s_out, BODY * i + j + 1)
                sp.dma_start(out[BODY * i + j], o[j // 2 % 2][j % 2]).then_inc(s_store[j % 4], 16)
                if more:
                    sp.dma_start(xring[:, j, :], x[BODY * (i + 1) + j]).then_inc(s_x2[j], 16)

            with sp.Fori(0, TRIPS - 1) as i:
                for j in range(BODY):
                    store_and_reload(i, j, True)
            for j in range(BODY):
                store_and_reload(TRIPS - 1, j, False)
            for q in s_store:
                sp.wait_ge(q, 16 * (B // 4 + 1))

        @block.gpsimd
        def _(pool):
            nc.gpsimd.memset(neg_half[:], -0.5).then_inc(s_pchain, 1)
            nc.gpsimd.memset(eps[:], EPS).then_inc(s_pchain, 1)
            nc.gpsimd.memset(minus_one[:], -1.0).then_inc(s_pchain, 1)
            nc.gpsimd.memset(acc, 0.0).then_inc(s_pchain, 1)
            nc.gpsimd.memset(ones[:], 1.0).then_inc(s_pchain, 1)
            pool.wait_ge(s_pchain, 5)
            nc.gpsimd.affine_select(out=ident[:], in_=ones[:], compare_op=ALU.is_equal, fill=0.0, base=0,
                                    pattern=[[-1, P]], channel_multiplier=1).then_inc(s_ident, 1)
            pool.wait_ge(s_ident, 1)
            nc.gpsimd.tensor_copy(ident16[:], ident[:]).then_inc(s_ident, 1)

            def norms(i, g):
                i, g = i + g // NG, g % NG
                a, n = NORM_GROUPS[g]
                done = 5 + 3 * (NG * i + g)
                pool.wait_ge(s_mom, BODY1 * i + a + n)
                nc.gpsimd.tensor_tensor(var_eps[:, 0:n], moments[:, a:a + n, 1], eps[:, 0:n],
                                        ALU.add).then_inc(s_pchain, 1)
                nc.gpsimd.tensor_tensor(neg_mean[:, 0:n], moments[:, a:a + n, 0], minus_one[:, 0:n],
                                        ALU.mult).then_inc(s_pchain, 1)
                pool.wait_ge(s_pchain, done + 2)
                r = rstd[:, bass.ds(BODY1 * i + a, n)]
                nc.gpsimd.tensor_tensor(r, var_eps[:, 0:n], neg_half[:, 0:n], ALU.pow).then_inc(s_pchain, 1)
                pool.wait_ge(s_pchain, done + 3)
                nc.gpsimd.tensor_tensor(nbias[:, bass.ds(BODY1 * i + a, n)], neg_mean[:, 0:n], r,
                                        ALU.mult).then_inc(s_norm, 1)
                pool.wait_ge(s_norm, NG * (i + 1) + g + 1)

            def add(i, j):
                k = POOL_SUMS.index(j)
                pool.wait_ge(s_h, BODY1 * i + j + 1)
                pool.wait_ge(s_hpool, NP * (i + 1) + k)
                nc.gpsimd.tensor_tensor(acc, acc, h1[j % HS], ALU.add).then_inc(s_hpool, 1)

            pool.sem_inc(s_hpool, NP)
            pool.sem_inc(s_norm, NG)

            def sums(i, more, except_for=()):
                for g, (a, n) in enumerate(NORM_GROUPS):
                    if more or g + 1 < NG:
                        norms(i, g + 1)
                    for j in range(a, a + n):
                        if j in POOL_SUMS and j not in except_for:
                            add(i, j)

            norms(0, 0)
            with pool.Fori(0, TRIPS1 - 1) as i:
                sums(i, True)
            sums(TRIPS1 - 1, False, VECTOR_SUMS)

            pool.wait_ge(s_n2s, 1)
            nc.gpsimd.tensor_tensor(rnorm[:], norm2[:], neg_half[:], ALU.pow).then_inc(s_rn, 1)
            for c in range(C):
                pool.wait_ge(s_sims, c + 1)
                pool.wait_ge(s_gum[c], 16)
                if c >= 2:
                    pool.wait_ge(s_adj, c - 1)
                nc.gpsimd.tensor_tensor(score0[c % 2], sim_s[c % 2],
                                        gum[:, c % GUMBEL_SLOTS, :].rearrange("p (d g) -> p g d", g=2)[:, 0, :],
                                        ALU.add).then_inc(s_sc0, 1)
            for e in range(C):
                c = e // 2
                if e < C - 1:
                    pool.wait_ge(s_cm, e + 1)
                    pool.wait_ge(s_com2, e + 1)
                    nc.gpsimd.tensor_tensor(a32(e), com2[e % 4], cmask[e % 4], ALU.mult).then_inc(s_a32, 1)
                if e % 2 == 1:
                    pool.wait_ge(s_a32, e + 1)
                    if c >= 2:
                        pool.wait_ge(s_alo, 3 * (c - 1))
                    nc.gpsimd.tensor_tensor(t32[c % 2][:, 2, :], a32(e)[:, HI], a32(e - 1)[:, HI],
                                            ALU.subtract).then_inc(s_t3, 1)
                if 1 <= e < SUMMED:
                    pool.wait_ge(s_a32, e + 1)
                    if e >= 2:
                        pool.wait_ge(s_asum, e - 1)
                    nc.gpsimd.tensor_tensor(asum, a32(0) if e == 1 else asum, a32(e), ALU.add).then_inc(s_asum, 1)
            pool.wait_ge(s_dchain, 4)
            nc.gpsimd.tensor_tensor(dinv_raw[:], degree[:], neg_half[:], ALU.pow).then_inc(s_pow, 1)
            for c, t in ((HC - 2, 2), (HC - 1, 0)):
                pool.wait_ge(s_ahi, 3 * c + 3)
                nc.gpsimd.tensor_tensor(a16[:, 1, 3 + t:7, c, :], t32[c % 2][:, t:4, :], a16[:, 0, 3 + t:7, c, :],
                                        ALU.subtract)

            with pool.Fori(0, TRIPS * PAIRS) as r:
                pool.wait_ge(s_z, 2 * r + 2)
                pool.wait_ge(s_y, 4 * r + 4)
                nc.gpsimd.tensor_tensor(z[:, 4, :], z[:, 0, :], z[:, 3, :], ALU.add).then_inc(s_zs, 1)
                pool.wait_ge(s_zs, 4 * r + 1)
                nc.gpsimd.tensor_tensor(z[:, 5, :], z[:, 4, :], z[:, 1, :], ALU.subtract).then_inc(s_zs, 1)
                nc.gpsimd.tensor_tensor(z[:, 6, :], z[:, 1, :], z[:, 0, :], ALU.subtract).then_inc(s_zs, 1)
                pool.wait_ge(s_zs, 4 * r + 2)
                nc.gpsimd.tensor_tensor(z[:, 7, :], z[:, 2, :], z[:, 5, :], ALU.subtract).then_inc(s_zs, 1)

        @block.scalar
        def _(act):
            def relu1(i, j):
                act.wait_ge(s_norm, NG * (i + 1) + norm_group(j) + 1)
                last = (j + BODY1 - HS) % BODY1
                trip = i + 1 if j >= HS else i
                if last in POOL_SUMS:
                    act.wait_ge(s_hpool, NP * trip + POOL_SUMS.index(last) + 1)
                else:
                    act.wait_ge(s_hpe, NT * trip + TENSOR_SUMS.index(last) + 1)
                t = BODY1 * i + j
                nc.scalar.activation(h1[j % HS], x1[j], ACT.Relu, bias=nbias[:, bass.ds(t, 1)],
                                     scale=rstd[:, bass.ds(t, 1)]).then_inc(s_h, 1)

            def keep(n):
                act.wait_ge(s_xw1, n + 1)
                nc.scalar.activation(xw_res[:, bass.ds(n, 1), :].rearrange("p a n -> p (a n)"),
                                     ps_xw1, ACT.Copy).then_inc(s_xw1used, 1)

            act.wait_ge(s_wchain, 5)
            nc.scalar.activation(w_unit[:], w_inv[:], ACT.Copy).then_inc(s_w, 1)
            act.sem_inc(s_xw1used, 1)
            with act.Fori(0, TRIPS1) as i:
                for j in range(BODY1):
                    relu1(i, j)
                    if j in KEEP_AFTER:
                        keep(NK * i + KEEP_AFTER.index(j))

            for half, m in enumerate((LO, HI)):
                act.wait_ge(s_S, half + 1)
                nc.scalar.activation(sq[:, m], S[:, m], ACT.Square, scale=1.0 / B).then_inc(s_sq, 1)
            for c in range(C):
                act.wait_ge(s_sim, c + 1)
                if c >= 2:
                    act.wait_ge(s_sc0, c - 1)
                    act.wait_ge(s_sc1, c - 1)
                nc.scalar.activation(sim_s[c % 2], ps_sim[c % 2], ACT.Copy, bias=0.5,
                                     scale=0.5).then_inc(s_sims, 1)
            for c in range(0, C, 2):
                act.wait_ge(s_sym, c + 1)
                nc.scalar.activation(nmask[:, c, :], ps_sym[c % 4], ACT.Sign,
                                     accum_out=row_count[:, c:c + 1]).then_inc(s_mask[0], 1)

            def high_a(c):
                act.wait_ge(s_a32, 2 * c + 2)
                nc.scalar.activation(a16[:, 0, 0, c, :], a32(2 * c)[:, LO], ACT.Copy).then_inc(s_ahi, 1)
                nc.scalar.activation(a16[:, 0, 1:3, c, :], a32(2 * c + 1).rearrange("p (a n) -> p a n", a=2),
                                     ACT.Copy).then_inc(s_ahi, 1)

            def high_t(c):
                act.wait_ge(s_ts, 3 * (c + 1))
                act.wait_ge(s_t3, c + 1)
                nc.scalar.activation(a16[:, 0, 3:7, c, :], t32[c % 2], ACT.Copy).then_inc(s_ahi, 1)

            for e in range(C):
                act.wait_ge(s_com, e + 1)
                if e >= 4:
                    act.wait_ge(s_a32, e - 3)
                nc.scalar.activation(com2[e % 4], ps_com[e % 3], ACT.Square,
                                     scale=COMMON_SCALE).then_inc(s_com2, 1)
                if e >= 2 and e % 2 == 0:
                    high_a(e // 2 - 1)
                if e >= 3 and e % 2 == 1:
                    high_t(e // 2 - 1)
            high_a(HC - 1)

            def relu2(i, q, b):
                i, q = i + q // PAIRS, q % PAIRS
                j = 2 * q + b
                if j == RESIDENT:
                    return
                n = (BODY - 1) * i + j - 1
                act.wait_ge(s_x2[j], 16 * (i + 1))
                act.wait_ge(s_hlo, n + 1)
                back = (3 if q == 1 else 2) if b == 0 else (1 if q == 0 else 2)
                act.wait_ge(s_xw2, n + 3 - back)
                t = BODY * i + j
                bias, scale = nbias[:, bass.ds(t, 1)], rstd[:, bass.ds(t, 1)]
                nc.scalar.activation(h32, xring[:, j, :], ACT.Relu, bias=bias, scale=scale).then_inc(s_h32, 1)
                nc.scalar.activation(h16[b][:, 0, :], xring[:, j, :], ACT.Relu, bias=bias,
                                     scale=scale).then_inc(s_hhi, 1)

            def y_high(i, q, g):
                i, q = i + q // PAIRS, q % PAIRS
                r = PAIRS * i + q
                if g == 0:
                    act.wait_ge(s_z, 2 * r + 1)
                    act.wait_ge(s_mm, 7 * (r + 1))
                elif g == 1:
                    act.wait_ge(s_z, 2 * r + 2)
                else:
                    act.wait_ge(s_zs, 4 * r + 2 * g - 2)
                a, n = GROUPS[g]
                nc.scalar.activation(y16[:, q % 2, 0, a:a + n, :], z[:, a + 1:a + 1 + n, :],
                                     ACT.Copy).then_inc(s_yhi, 1)

            def partial(i, q, k):
                r = PAIRS * i + q
                if k == 0:
                    act.wait_ge(s_store[2 * (q % 2)], 16 * ((PAIRS // 2) * i + q // 2 + 1))
                    act.wait_ge(s_store[2 * (q % 2) + 1], 16 * ((PAIRS // 2) * i + q // 2 + 1))
                if k == 1:
                    act.wait_ge(s_c22, r + 1)
                act.wait_ge(s_mm, 14 + 7 * r + (1, 2, 3, 5)[k])
                dst = (o[q % 2][0][:, 0:H], p5[:], o[q % 2][0][:, H:N], o[q % 2][1][:, H:N])[k]
                src = (ps_b, ps_d, ps_b, ps_b)[k][q % 2]
                nc.scalar.activation(dst, src, ACT.Copy).then_inc(s_v, 1)

            def act_pair(i, q, ahead1, ahead2):
                partial(i, q, 0)
                if ahead1:
                    y_high(i, q + 1, 0)
                partial(i, q, 1)
                if ahead2:
                    relu2(i, q + 2, 0)
                partial(i, q, 2)
                if ahead1:
                    y_high(i, q + 1, 1)
                if ahead2:
                    relu2(i, q + 2, 1)
                if ahead1:
                    y_high(i, q + 1, 2)
                partial(i, q, 3)
                if ahead1:
                    y_high(i, q + 1, 3)

            act.wait_ge(s_alo, 3 * 2)
            act.wait_ge(s_asum, SUMMED - 1)
            relu2(0, 0, 1)
            high_t(HC - 1)
            y_high(0, 0, 0)
            relu2(0, 1, 0)
            y_high(0, 0, 1)
            y_high(0, 0, 2)
            relu2(0, 1, 1)
            y_high(0, 0, 3)
            with act.Fori(0, TRIPS - 1) as i:
                for q in range(PAIRS):
                    act_pair(i, q, True, True)
            for q in range(PAIRS):
                act_pair(TRIPS - 1, q, q + 1 < PAIRS, q + 2 < PAIRS)

        @block.tensor
        def _(pe):
            pe.sem_inc(s_hpe, NT)
            pe.sem_inc(s_mm, 14)
            pe.sem_inc(s_xw2, 2)
            pe.wait_ge(s_wabs, 1)
            pe.wait_ge(s_ident, 2)
            nc.tensor.matmul(ps_w[:, 0:P], ones[:], w_abs[:], start=True, stop=True)
            nc.tensor.matmul(ps_w[:, P:P + 1], w_abs[:], ones[:, 0:1], start=True, stop=True,
                             skip_group_check=True).then_inc(s_wsum, 1)
            for m in range(2):
                nc.tensor.matmul(ps_avg[:, m * H:m * H + P], zeros[:], ones[:], start=True, stop=True,
                                 skip_group_check=True)

            def stay_awake(dst, n, start=True):
                for _ in range(n):
                    nc.tensor.matmul(dst, zeros[:], ones[:], start=start, stop=True, skip_group_check=True)

            def bcast(dst, col, half):
                for c in range(half * HC, (half + 1) * HC):
                    mm = nc.tensor.matmul(dst[:, c * P:(c + 1) * P], col[:, c:c + 1].broadcast_to([P, P]), ident[:],
                                          start=True, stop=True, skip_group_check=True)
                return mm

            pe.wait_ge(s_w, 1)
            def sums(i, except_for=()):
                for j in range(BODY1):
                    h = h1[j % HS]
                    if j in KEPT:
                        pe.wait_ge(s_h, BODY1 * i + j + 1)
                        pe.wait_ge(s_xw1used, NK * i + KEPT.index(j) + 1)
                        for c in range(C):
                            mm = nc.tensor.matmul(ps_xw1[:, c * P:(c + 1) * P], h[:, c * P:(c + 1) * P], w_unit[:],
                                                  start=True, stop=True, skip_group_check=True)
                        mm.then_inc(s_xw1, 1)
                    if j in TENSOR_SUMS and j not in except_for:
                        pe.wait_ge(s_h, BODY1 * i + j + 1)
                        for m in (LO, HI):
                            mm = nc.tensor.matmul(ps_avg[:, m], ident[:], h[:, m], start=False, stop=True,
                                                  skip_group_check=True)
                        mm.then_inc(s_hpe, 1)

            with pe.Fori(0, TRIPS1 - 1) as i:
                sums(i)
            sums(TRIPS1 - 1, VECTOR_SUMS)

            stay_awake(ps[:, 6, 2 * P:3 * P], 12)
            for c in range(C):
                pe.wait_ge(s_sq, c // HC + 1)
                mm = nc.tensor.matmul(ps_norm[:, c:c + 1], sq[:, c * P:(c + 1) * P], ones[:, 0:1],
                                      start=True, stop=True, skip_group_check=True)
            mm.then_inc(s_n2, 1)
            stay_awake(ps[:, 7, 2 * P:3 * P], 7)
            pe.wait_ge(s_rn, 1)
            for half in (0, 1):
                bcast(ps_bc, rnorm, half).then_inc(s_bc, 1)
            for c in range(C):
                if c >= 2:
                    pe.wait_ge(s_sims, c - 1)
                for m in range(2):
                    if c == 0:
                        pe.wait_ge(s_xn, m + 1)
                    mm = nc.tensor.matmul(ps_sim[c % 2][:, m * H:(m + 1) * H], xn[:, c * P:(c + 1) * P],
                                          xn[:, m * H:(m + 1) * H], start=True, stop=True)
                mm.then_inc(s_sim, 1)

            def sym_start(c):
                for m in (LO, HI):
                    nc.tensor.matmul(ps_sym[c % 4][:, m], ident16[:], adjm[:, c, m], start=True, stop=False,
                                     skip_group_check=True)
                nc.tensor.matmul(ps_sym[c % 4][:, c * P:(c + 1) * P], ident16[:], ident16[:],
                                 start=False, stop=False, skip_group_check=True)

            def sym_part(c, k):
                return nc.tensor.matmul(ps_sym[c % 4][:, k * P:(k + 1) * P], adjm[:, k, c * P:(c + 1) * P], ident16[:],
                                        start=False, stop=True, skip_group_check=True)

            for k in range(C):
                pe.wait_ge(s_adj, k + 1)
                if k < 2:
                    sym_start(k)
                if k == 1:
                    sym_part(0, 0)
                    sym_part(1, 0)
                if k >= 1:
                    for c in (0, 1):
                        mm = sym_part(c, k)
                        if k == C - 1:
                            mm.then_inc(s_sym, 1)
                if k < C - 1:
                    stay_awake(ps_sym[0][:, 0:P], 3, start=False)
            for c in range(2, C):
                if c >= 4:
                    pe.wait_ge(s_mask[c % 2], c // 2 - 1)
                sym_start(c)
                for k in range(C):
                    mm = sym_part(c, k)
                mm.then_inc(s_sym, 1)

            def degrees(e):
                if e == SUMMED - 1:
                    pe.wait_ge(s_asum, SUMMED - 1)
                else:
                    pe.wait_ge(s_a32, e + 1)
                src = asum if e == SUMMED - 1 else a32(e)
                for d in range(C):
                    mm = nc.tensor.matmul(ps_deg[:, d:d + 1], src[:, d * P:(d + 1) * P], ones[:, 0:1],
                                          start=(e == SUMMED - 1 and d == 0), stop=(e == C - 1), skip_group_check=True)
                mm.then_inc(s_dsum, 1)

            def turn(n):
                pe.wait_ge(s_colmax, n + 1)
                nc.tensor.transpose(ps_top[0:1, 0:P], col2[:, n:n + 1], ident[:]).then_inc(s_topT, 1)

            def spread(n):
                pe.wait_ge(s_top, n + 1)
                nc.tensor.matmul(ps_top[:, P:P + 1], ones[0:1, :], top[:, n:n + 1], start=True, stop=True,
                                 skip_group_check=True).then_inc(s_topb, 1)

            pe.wait_ge(s_mask[1], 3)
            DEGREES_AFTER = {C - 3: (SUMMED - 1, SUMMED), C - 2: (C - 4,), C - 1: (C - 3, C - 2, C - 1)}
            for e, c in enumerate(CHUNKS):
                if e >= 3:
                    pe.wait_ge(s_com2, e - 2)
                for k in range(C):
                    if e == 0:
                        for n in {c % 2, k % 2}:
                            pe.wait_ge(s_mask[n], max(c, k) // 2 + 1)
                    for m in range(2):
                        mm = nc.tensor.matmul(ps_com[e % 3][:, m * H:(m + 1) * H], nmask[:, k, c * P:(c + 1) * P],
                                              nmask[:, k, m * H:(m + 1) * H], start=(k == 0), stop=(k == C - 1))
                mm.then_inc(s_com, 1)
                if e == 0:
                    turn(0)
                if e == 1:
                    spread(0)
                for n in DEGREES_AFTER.get(e, ()):
                    degrees(n)
            turn(1)
            spread(1)

            def xw_of(i, q, b):
                i, q = i + q // PAIRS, q % PAIRS
                j = 2 * q + b
                if j == RESIDENT:
                    return
                pe.wait_ge(s_hlo, (BODY - 1) * i + j + 1)
                if j > 1 or not isinstance(i, int) or i > 0:
                    pe.wait_ge(s_z, BODY * i + j)
                for c in range(C):
                    for hk, wk in ((0, 0), (0, 1), (1, 0)):
                        mm = nc.tensor.matmul(ps_xw2[:, c * P:(c + 1) * P], h16[b][:, hk, c * P:(c + 1) * P],
                                              w16[:, wk, :], start=(hk == wk == 0), stop=(hk == 1),
                                              skip_group_check=True)
                mm.then_inc(s_xw2, 1)

            def product(q, u, mat, bank, start):
                for c in range(HC):
                    for yk, ak in ((0, 0), (0, 1), (1, 0)):
                        mm = nc.tensor.matmul(bank[q % 2], y16[:, q % 2, yk, u, c * P:(c + 1) * P],
                                              a16[:, ak, mat, c, :], start=(start and c == yk == ak == 0),
                                              stop=(c == HC - 1 and yk == 1), skip_group_check=True)
                mm.then_inc(s_mm, 1)

            def pe_pair(i, q, ahead1):
                r = PAIRS * i + q
                pe.wait_ge(s_y, 4 * r + 5)
                pe.wait_ge(s_c, 3 * r + 3)
                product(q, 0, 0, ps_b, True)
                if ahead1:
                    xw_of(i, q + 1, 0)
                pe.wait_ge(s_y, 4 * r + 7)
                product(q, 3, 3, ps_d, True)
                pe.wait_ge(s_v, 4 * r + 1)
                product(q, 4, 4, ps_b, False)
                if ahead1:
                    xw_of(i, q + 1, 1)
                pe.wait_ge(s_y, 4 * r + 8)
                pe.wait_ge(s_v, 4 * r + 2)
                product(q, 6, 2, ps_d, False)
                pe.wait_ge(s_v, 4 * r + 3)
                product(q, 5, 5, ps_b, False)
                product(q, 1, 1, ps_a, True)
                pe.wait_ge(s_v, 4 * r + 4)
                product(q, 2, 6, ps_b, False)

            xw_of(0, 0, 1)
            pe.wait_ge(s_dchain, 10)
            for half in (0, 1):
                bcast(ps_rowf, row_f, half).then_inc(s_rowp, 1)
            with pe.Fori(0, TRIPS - 1) as i:
                for q in range(PAIRS):
                    pe_pair(i, q, True)
            for q in range(PAIRS):
                pe_pair(TRIPS - 1, q, q + 1 < PAIRS)

        @block.vector
        def _(dve):
            dve.sem_inc(s_c, 6)
            dve.sem_inc(s_y, 4)
            dve.sem_inc(s_hlo, 1)
            dve.sem_inc(s_c22, 1)
            nc.vector.memset(zeros[:], 0.0).then_inc(s_wchain, 1)
            dve.wait_ge(s_consts, 32)
            nc.vector.scalar_tensor_tensor(out=w_abs[:], in0=w[:], scalar=-1.0, in1=w[:], op0=ALU.mult,
                                           op1=ALU.max).then_inc(s_wabs, 1)
            dve.wait_ge(s_wsum, 1)
            nc.vector.tensor_scalar(w_inv[:], ps_w[:, 0:P], TINY, None, ALU.max).then_inc(s_wchain, 1)
            nc.vector.tensor_scalar(w_sum[:], ps_w[:, P:P + 1], TINY, None, ALU.max).then_inc(s_wchain, 1)
            dve.wait_ge(s_wchain, 3)
            nc.vector.reciprocal(w_unit[:], w_inv[:]).then_inc(s_wchain, 1)
            dve.wait_ge(s_wchain, 4)
            nc.vector.scalar_tensor_tensor(out=w_inv[:], in0=w_unit[:], scalar=W_SCALE, in1=w[:], op0=ALU.mult,
                                           op1=ALU.mult).then_inc(s_wchain, 1)
            dve.wait_ge(s_wchain, 5)
            nc.vector.tensor_copy(w16[:, 0, :], w_inv[:]).then_inc(s_wchain, 1)
            dve.wait_ge(s_wchain, 6)
            nc.vector.tensor_tensor(w16[:, 1, :], w_inv[:], w16[:, 0, :], ALU.subtract).then_inc(s_wchain, 1)

            with dve.Fori(0, TRIPS1) as i:
                for q in range(BODY1 // 2):
                    for j in (2 * q, 2 * q + 1):
                        dve.wait_ge(s_x1[j], 16 * (i + 1))
                        for m in range(2):
                            nc.vector.bn_stats(stats[:, j % 4, 6 * m:6 * m + 6],
                                               x1[j][:, m * H:(m + 1) * H]).then_inc(s_bn, 1)
                    dve.wait_ge(s_norm, NG * i + norm_group(2 * q) + 1)
                    dve.wait_ge(s_bn, 2 * (BODY1 * i + 2 * q) + 4)
                    dve.sem_inc(s_bnseen, 1)
                    for j in (2 * q, 2 * q + 1):
                        nc.vector.bn_aggr(moments[:, j, :], stats[:, j % 4, :]).then_inc(s_mom, 1)

            mine = h1[VECTOR_SUMS[0] % HS]
            dve.wait_ge(s_h, B - BODY1 + VECTOR_SUMS[0] + 1)
            for n, j in enumerate(VECTOR_SUMS[1:]):
                dve.wait_ge(s_h, B - BODY1 + j + 1)
                if n >= 1:
                    dve.wait_ge(s_mine, n)
                nc.vector.tensor_tensor(mine, mine, h1[j % HS], ALU.add).then_inc(s_mine, 1)
            mine_pool = sum(j in POOL_SUMS for j in VECTOR_SUMS)
            dve.wait_ge(s_mine, len(VECTOR_SUMS) - 1)
            dve.wait_ge(s_hpool, NP * (TRIPS1 + 1) - mine_pool)
            nc.vector.tensor_tensor(mine, mine, acc, ALU.add).then_inc(s_mine, 1)
            dve.wait_ge(s_mine, len(VECTOR_SUMS))
            dve.wait_ge(s_hpe, NT * (TRIPS1 + 1) - len(VECTOR_SUMS) + mine_pool)
            for m in (LO, HI):
                nc.vector.tensor_tensor(S[:, m], ps_avg[:, m], mine[:, m], ALU.add).then_inc(s_S, 1)
            dve.wait_ge(s_n2, 1)
            nc.vector.tensor_scalar(norm2[:], ps_norm, NORM_MIN ** 2, None, ALU.max).then_inc(s_n2s, 1)

            for half, m in enumerate((LO, HI)):
                dve.wait_ge(s_bc, half + 1)
                dve.wait_ge(s_S, half + 1)
                nc.vector.scalar_tensor_tensor(out=xn[:, m], in0=S[:, m], scalar=1.0 / B, in1=ps_bc[:, m],
                                               op0=ALU.mult, op1=ALU.mult).then_inc(s_xn, 1)
            for c in range(C):
                dve.wait_ge(s_sims, c + 1)
                dve.wait_ge(s_gum[c], 16)
                if c >= 2:
                    dve.wait_ge(s_adj, c - 1)
                nc.vector.scalar_tensor_tensor(out=nscore1[c % 2], in0=sim_s[c % 2], scalar=1.0,
                                               in1=gum[:, c % GUMBEL_SLOTS, :].rearrange("p (d g) -> p g d", g=2)[:, 1, :],
                                               op0=ALU.subtract, op1=ALU.subtract).then_inc(s_sc1, 1)
                dve.wait_ge(s_sc1, c + 1)
                dve.wait_ge(s_sc0, c + 1)
                nc.vector.scalar_tensor_tensor(out=adjm[:, c, :], in0=nscore1[c % 2], scalar=-1.0, in1=score0[c % 2],
                                               op0=ALU.mult, op1=ALU.is_lt).then_inc(s_adj, 1)

            for c in range(1, C, 2):
                dve.wait_ge(s_sym, c + 1)
                nc.vector.tensor_scalar(nmask[:, c, :], ps_sym[c % 4], 1.0, 0.0, ALU.min, ALU.add,
                                        accum_out=row_count[:, c:c + 1]).then_inc(s_mask[1], 1)
            for k in (0, 1):
                dve.wait_ge(s_mask[k], C // 2)
            nc.vector.tensor_reduce(col2[:, 0:1], row_count[:], AX_X, ALU.max).then_inc(s_colmax, 1)

            def top_of(n):
                dve.wait_ge(s_topT, n + 1)
                nc.vector.tensor_reduce(top[:, n:n + 1], ps_top[0:1, 0:P], AX_X, ALU.max).then_inc(s_top, 1)

            def ts(c):
                t = t32[c % 2]
                dve.wait_ge(s_a32, 2 * c + 2)
                if c >= 2:
                    dve.wait_ge(s_alo, 3 * (c - 1))
                a11, a12, a21, a22 = (a32(2 * c + k)[:, m] for k in (0, 1) for m in (LO, HI))
                nc.vector.tensor_tensor(t[:, 0, :], a12, a11, ALU.subtract).then_inc(s_ts, 1)
                dve.wait_ge(s_ts, 3 * c + 1)
                nc.vector.tensor_tensor(t[:, 1, :], a22, t[:, 0, :], ALU.subtract).then_inc(s_ts, 1)
                dve.wait_ge(s_ts, 3 * c + 2)
                nc.vector.tensor_tensor(t[:, 3, :], a21, t[:, 1, :], ALU.subtract).then_inc(s_ts, 1)

            def low_a11(c):
                dve.wait_ge(s_ahi, 3 * c + 1)
                nc.vector.tensor_tensor(a16[:, 1, 0, c, :], a32(2 * c)[:, LO], a16[:, 0, 0, c, :],
                                        ALU.subtract).then_inc(s_alo, 1)

            def low_a2(c):
                dve.wait_ge(s_ahi, 3 * c + 2)
                nc.vector.tensor_tensor(a16[:, 1, 1:3, c, :], a32(2 * c + 1).rearrange("p (a n) -> p a n", a=2),
                                        a16[:, 0, 1:3, c, :], ALU.subtract).then_inc(s_alo, 1)

            def low_t(c):
                dve.wait_ge(s_ahi, 3 * c + 3)
                nc.vector.tensor_tensor(a16[:, 1, 3:7, c, :], t32[c % 2], a16[:, 0, 3:7, c, :],
                                        ALU.subtract).then_inc(s_alo, 1)

            def h_low(i, q, b):
                i, q = i + q // PAIRS, q % PAIRS
                j = 2 * q + b
                if j == RESIDENT:
                    return
                n = (BODY - 1) * i + j - 1
                dve.wait_ge(s_h32, n + 1)
                dve.wait_ge(s_hhi, n + 1)
                nc.vector.tensor_tensor(h16[b][:, 1, :], h32, h16[b][:, 0, :], ALU.subtract).then_inc(s_hlo, 1)

            for e, c in enumerate(CHUNKS):
                dve.wait_ge(s_com2, e + 1)
                if e >= 4:
                    dve.wait_ge(s_a32, e - 3)
                nc.vector.scalar_tensor_tensor(out=cmask[e % 4], in0=com2[e % 4], scalar=COMMON_SCALE ** 2,
                                               in1=adjm[:, c, :], op0=ALU.is_gt, op1=ALU.mult).then_inc(s_cm, 1)
                if e == 0:
                    top_of(0)
                if e == 1:
                    dve.wait_ge(s_topb, 1)
                    nc.vector.tensor_copy(top_b[:, 0:1], ps_top[:, P:P + 1]).then_inc(s_dchain, 1)
                    dve.wait_ge(s_dchain, 1)
                    nc.vector.reciprocal(small[:, 0:1], top_b[:, 0:1]).then_inc(s_dchain, 1)
                    dve.wait_ge(s_dchain, 2)
                    nc.vector.tensor_scalar(small[:, 1:2], small[:, 0:1], COMMON_SCALE ** -2, None,
                                            ALU.mult).then_inc(s_dchain, 1)
                if e >= 2 and e % 2 == 0:
                    ts(e // 2 - 1)
                if e >= 3 and e % 2 == 1 and e < C - 1:
                    low_a11(e // 2 - 1)
                    low_a2(e // 2 - 1)
                    low_t(e // 2 - 1)
            dve.wait_ge(s_a32, C - 1)
            dve.wait_ge(s_cm, C)
            nc.vector.tensor_tensor(a32(C - 1), com2[(C - 1) % 4], cmask[(C - 1) % 4],
                                    ALU.mult).then_inc(s_a32, 1)
            low_a11(HC - 2)
            low_a2(HC - 2)
            dve.wait_ge(s_ahi, 3 * (HC - 2) + 3)
            nc.vector.tensor_tensor(a16[:, 1, 3:5, HC - 2, :], t32[HC % 2][:, 0:2, :], a16[:, 0, 3:5, HC - 2, :],
                                    ALU.subtract).then_inc(s_alo, 1)
            dve.wait_ge(s_dchain, 3)
            dve.wait_ge(s_dsum, C - SUMMED + 1)
            nc.vector.tensor_scalar(degree[:], ps_deg, small[:, 1:2], TINY, ALU.mult, ALU.max).then_inc(s_dchain, 1)
            nc.vector.tensor_scalar(has_deg[:], ps_deg, 0.0, None, ALU.is_gt).then_inc(s_dchain, 1)
            ts(HC - 1)
            dve.wait_ge(s_pow, 1)
            dve.wait_ge(s_dchain, 5)
            nc.vector.tensor_tensor(dinv[:], dinv_raw[:], has_deg[:], ALU.mult).then_inc(s_dchain, 1)
            dve.wait_ge(s_dchain, 6)
            nc.vector.tensor_reduce(col2[:, 1:2], dinv[:], AX_X, ALU.max).then_inc(s_colmax, 1)
            top_of(1)
            h_low(0, 0, 1)
            dve.wait_ge(s_topb, 2)
            nc.vector.tensor_scalar(top_b[:, 1:2], ps_top[:, P:P + 1], TINY, None, ALU.max).then_inc(s_dchain, 1)
            dve.wait_ge(s_dchain, 7)
            nc.vector.reciprocal(small[:, 2:3], top_b[:, 1:2]).then_inc(s_dchain, 1)
            dve.wait_ge(s_dchain, 8)
            nc.vector.tensor_scalar(u[:], dinv[:], small[:, 2:3], Y_SCALE / W_SCALE, ALU.mult, ALU.mult).then_inc(s_u, 1)
            nc.vector.tensor_scalar(small[:, 3:4], top_b[:, 1:2], small[:, 1:2], 1.0 / Y_SCALE,
                                    ALU.mult, ALU.mult).then_inc(s_dchain, 1)
            dve.wait_ge(s_dchain, 9)
            nc.vector.tensor_scalar(row_f[:], dinv[:], small[:, 3:4], None, ALU.mult).then_inc(s_dchain, 1)
            dve.wait_ge(s_u, 1)

            def z_of(i, q, b):
                i, q = i + q // PAIRS, q % PAIRS
                j, r = 2 * q + b, PAIRS * i + q
                if b == 0:
                    dve.wait_ge(s_y, 4 * r + 4)
                if j == RESIDENT:
                    src = xw_res[:, bass.ds(i, 1), :].rearrange("p a (m c t) -> p (a m) c t", m=2, c=HC)
                else:
                    dve.wait_ge(s_xw2, (BODY - 1) * i + j + 2)
                    src = ps_xw2.rearrange("p (m c t) -> p m c t", m=2, c=HC)
                dst = z[:, 1:3, :] if b == 0 else z[:, 0:4:3, :]
                nc.vector.tensor_tensor(dst.rearrange("p m (c t) -> p m c t", c=HC), src,
                                        u[:].rearrange("p (m c) -> p m c", m=2).unsqueeze(3).broadcast_to(
                                            [P, 2, HC, P]), ALU.mult).then_inc(s_z, 1)

            def y_low(i, q, g):
                i, q = i + q // PAIRS, q % PAIRS
                dve.wait_ge(s_yhi, 4 * (PAIRS * i + q) + g + 1)
                a, n = GROUPS[g]
                nc.vector.tensor_tensor(y16[:, q % 2, 1, a:a + n, :], z[:, a + 1:a + 1 + n, :],
                                        y16[:, q % 2, 0, a:a + n, :], ALU.subtract).then_inc(s_y, 1)

            def scale(dst, src, cols):
                return nc.vector.scalar_tensor_tensor(out=dst, in0=src, scalar=w_sum[:, 0:1], in1=row_fb[:, cols],
                                                      op0=ALU.mult, op1=ALU.mult)

            def finish(i, q, b):
                j, ob = 2 * q + b, o[q % 2][b]
                dve.wait_ge(s_x2[j], 16 * (i + 1))
                nc.vector.scalar_tensor_tensor(out=ob, in0=ob, scalar=bias_sb[:, 0:1], in1=xring[:, j, :],
                                               op0=ALU.add, op1=ALU.add).then_inc(s_out, 1)

            def dve_pair(i, q, ahead1, ahead2):
                r = PAIRS * i + q
                o0, o1 = o[q % 2]
                if ahead1:
                    z_of(i, q + 1, 0)
                if ahead1:
                    y_low(i, q + 1, 0)
                if ahead2:
                    h_low(i, q + 2, 0)
                if ahead1:
                    z_of(i, q + 1, 1)
                    y_low(i, q + 1, 1)
                dve.wait_ge(s_mm, 14 + 7 * r + 4)
                dve.wait_ge(s_v, 4 * r + 3)
                nc.vector.tensor_tensor(o0[:, HI], ps_d[q % 2], o0[:, HI], ALU.add).then_inc(s_c, 1)
                if ahead2:
                    h_low(i, q + 2, 1)
                if ahead1:
                    y_low(i, q + 1, 2)
                dve.wait_ge(s_v, 4 * r + 4)
                nc.vector.tensor_tensor(o1[:, HI], o1[:, HI], p5[:], ALU.add).then_inc(s_c22, 1)
                dve.wait_ge(s_c22, r + 2)
                scale(o1[:, HI], o1[:, HI], HI).then_inc(s_scaled, 1)
                dve.wait_ge(s_mm, 14 + 7 * r + 6)
                nc.vector.tensor_tensor(o0[:, LO], ps_a[q % 2], o0[:, LO], ALU.add).then_inc(s_c, 1)
                if ahead1:
                    y_low(i, q + 1, 3)
                dve.wait_ge(s_c, 6 + 3 * r + 2)
                scale(o0, o0, slice(0, N)).then_inc(s_scaled, 1)
                dve.wait_ge(s_scaled, 2 * r + 2)
                finish(i, q, 0)
                dve.wait_ge(s_mm, 14 + 7 * r + 7)
                scale(o1[:, LO], ps_b[q % 2], LO).then_inc(s_c, 1)
                dve.wait_ge(s_c, 6 + 3 * r + 3)
                finish(i, q, 1)

            z_of(0, 0, 0)
            low_a11(HC - 1)
            z_of(0, 0, 1)
            y_low(0, 0, 0)
            h_low(0, 1, 0)
            y_low(0, 0, 1)
            low_a2(HC - 1)
            y_low(0, 0, 2)
            h_low(0, 1, 1)
            y_low(0, 0, 3)
            dve.wait_ge(s_rowp, 2)
            nc.vector.tensor_copy(row_fb, ps_rowf).then_inc(s_rowf, 1)
            dve.wait_ge(s_rowf, 1)
            with dve.Fori(0, TRIPS - 1) as i:
                for q in range(PAIRS):
                    dve_pair(i, q, True, True)
            for q in range(PAIRS):
                dve_pair(TRIPS - 1, q, q + 1 < PAIRS, q + 2 < PAIRS)


_INS = ["x", "adj", "L0_gnn_bias", "L0_gnn_gumbel"]
_OUTS = [((64, 128, 1024), "float32")]


def kernel(**inputs):
    import numpy as _np
    import concourse.bacc as _bacc
    from concourse import mybir as _mybir
    from concourse.bass_utils import run_bass_kernel_spmd as _run

    nc = _bacc.Bacc("TRN2", target_bir_lowering=False, num_devices=1)
    arrays, args = {}, []
    for name in _INS:
        a = _np.ascontiguousarray(inputs[name])
        arrays[f"in_{name}_dram"] = a
        args.append(nc.dram_tensor(f"in_{name}_dram", a.shape, _mybir.dt.from_np(a.dtype), kind="ExternalInput").ap())
    for i, (shape, dtype) in enumerate(_OUTS):
        dt = _mybir.dt.from_np(_np.dtype(dtype))
        args.append(nc.dram_tensor(f"out_{i}_dram", shape, dt, kind="ExternalOutput").ap())
    gnn_kernel(nc, *args)
    r = _run(nc, [arrays], core_ids=[0])
    got = tuple(r.results[0][f"out_{i}_dram"] for i in range(len(_OUTS)))
    return got[0]
```
